# Optimizing a Trainium2 kernel written in Bass

```python
import numpy as np
import jax
import jax.numpy as jnp

def _softmax(x, axis=-1):
    return jax.nn.softmax(x, axis=axis)

def _gelu(x):
    return jax.nn.gelu(x, approximate=True)

def _silu(x):
    return jax.nn.silu(x)

def _sigmoid(x):
    return jax.nn.sigmoid(x)

def _layernorm(x, axis=-1, eps=1e-05):
    m = jnp.mean(x, axis=axis, keepdims=True)
    v = jnp.var(x, axis=axis, keepdims=True)
    return (x - m) / jnp.sqrt(v + eps)

def _scatter_add(tgt, idx, src, axis=0):
    return tgt.at[idx].add(src)

def _segment_sum(src, seg, n):
    return jax.ops.segment_sum(src, seg, n)
kernel_name = 'mk_adaln_d1_jaxref_r8_5c7f53'

def setup_inputs(seed: int=0):
    np.random.seed(seed)
    _w = jnp.asarray

    def _L0_attn_setup():
        import jax, jax.numpy as jnp
        import numpy as np
        D_MODEL = 128
        N_HEADS = 16
        D_HEAD = D_MODEL // N_HEADS
        WINDOW = 32
        key = jax.random.key(seed)
        ks = jax.random.split(key, 9)
        x = jax.random.normal(ks[0], (1, 512, D_MODEL), dtype=jnp.float32)
        s = 0.02
        params = {'q_w': jax.random.normal(ks[1], (D_MODEL, D_MODEL), jnp.float32) * s, 'q_b': jax.random.normal(ks[2], (D_MODEL,), jnp.float32) * s, 'k_w': jax.random.normal(ks[3], (D_MODEL, D_MODEL), jnp.float32) * s, 'k_b': jax.random.normal(ks[4], (D_MODEL,), jnp.float32) * s, 'v_w': jax.random.normal(ks[5], (D_MODEL, D_MODEL), jnp.float32) * s, 'v_b': jax.random.normal(ks[6], (D_MODEL,), jnp.float32) * s, 'o_w': jax.random.normal(ks[7], (D_MODEL, D_MODEL), jnp.float32) * s, 'o_b': jax.random.normal(ks[8], (D_MODEL,), jnp.float32) * s}
        return {'x': x, **params}
    _L0_attn_in = _L0_attn_setup()

    def _L0_ffn_setup():
        import jax, jax.numpy as jnp
        import numpy as np
        E, K, D = (8, 2, 128)
        B, S = (2, 512)

        def _layernorm(x, g, b, eps=1e-06):
            m = jnp.mean(x, axis=-1, keepdims=True)
            v = jnp.var(x, axis=-1, keepdims=True)
            return (x - m) * jax.lax.rsqrt(v + eps) * g + b
        key = jax.random.key(seed)
        ks = jax.random.split(key, 6)
        n = lambda k, shape, scale: jax.random.normal(k, shape, jnp.float32) * scale
        return {'x': n(ks[0], (B, S, D), 1.0), 'gate_w': n(ks[1], (D, E), 0.02), 'w1': n(ks[2], (E, D, 2 * D), 0.02), 'b1': jnp.zeros((E, 2 * D), jnp.float32), 'w2': n(ks[3], (E, 2 * D, D), 0.02), 'b2': jnp.zeros((E, D), jnp.float32), 'ln_g': jnp.ones((E, D), jnp.float32), 'ln_b': jnp.zeros((E, D), jnp.float32)}
    _L0_ffn_in = _L0_ffn_setup()
    _L0_c = _w((lambda *s: np.random.randn(*s).astype(np.float32) * 0.05)(2, 128))
    _L0_wmod = _w((lambda *s: np.random.randn(*s).astype(np.float32) * 0.05)(128, 6 * 128) * 128 ** (-0.5))
    _d = {'L0_attn_x': _L0_attn_in['x'], 'L0_attn_q_w': _L0_attn_in['q_w'], 'L0_attn_q_b': _L0_attn_in['q_b'], 'L0_attn_k_w': _L0_attn_in['k_w'], 'L0_attn_k_b': _L0_attn_in['k_b'], 'L0_attn_v_w': _L0_attn_in['v_w'], 'L0_attn_v_b': _L0_attn_in['v_b'], 'L0_attn_o_w': _L0_attn_in['o_w'], 'L0_attn_o_b': _L0_attn_in['o_b'], 'L0_ffn_gate_w': _L0_ffn_in['gate_w'], 'L0_ffn_w1': _L0_ffn_in['w1'], 'L0_ffn_b1': _L0_ffn_in['b1'], 'L0_ffn_w2': _L0_ffn_in['w2'], 'L0_ffn_b2': _L0_ffn_in['b2'], 'L0_ffn_ln_g': _L0_ffn_in['ln_g'], 'L0_ffn_ln_b': _L0_ffn_in['ln_b'], 'L0_c': _L0_c, 'L0_wmod': _L0_wmod}
    _x0 = _d['L0_attn_x']
    _d['L0_attn_x'] = jax.random.normal(jax.random.fold_in(jax.random.key(seed), 1), (2, 1024, 128), dtype=_x0.dtype)
    del _x0
    return _d

def reference(L0_attn_x, L0_attn_q_w, L0_attn_q_b, L0_attn_k_w, L0_attn_k_b, L0_attn_v_w, L0_attn_v_b, L0_attn_o_w, L0_attn_o_b, L0_ffn_gate_w, L0_ffn_w1, L0_ffn_b1, L0_ffn_w2, L0_ffn_b2, L0_ffn_ln_g, L0_ffn_ln_b, L0_c, L0_wmod):

    def _L0_attn_ref(x, q_w, q_b, k_w, k_b, v_w, v_b, o_w, o_b):
        import jax, jax.numpy as jnp
        import numpy as np
        D_MODEL = 128
        N_HEADS = 16
        D_HEAD = D_MODEL // N_HEADS
        WINDOW = 32
        B, S, D = x.shape
        scale = jnp.sqrt(jnp.float32(D_HEAD))
        q = (x @ q_w.T + q_b).reshape(B, S, N_HEADS, D_HEAD).transpose(0, 2, 1, 3)
        k = (x @ k_w.T + k_b).reshape(B, S, N_HEADS, D_HEAD).transpose(0, 2, 1, 3)
        v = (x @ v_w.T + v_b).reshape(B, S, N_HEADS, D_HEAD).transpose(0, 2, 1, 3)
        scores = jnp.einsum('bhqd,bhkd->bhqk', q, k) / scale
        idx = jnp.arange(S)
        row = idx[:, None]
        col = idx[None, :]
        masked = (col > row) | (row - col >= min(WINDOW, S))
        scores = jnp.where(masked[None, None], -jnp.inf, scores)
        attn = jax.nn.softmax(scores, axis=-1)
        attn = jnp.nan_to_num(attn, nan=0.0)
        out = jnp.einsum('bhqk,bhkd->bhqd', attn, v)
        out = out.transpose(0, 2, 1, 3).reshape(B, S, D)
        return out @ o_w.T + o_b

    def _L0_ffn_ref(x, gate_w, w1, b1, w2, b2, ln_g, ln_b):
        import jax, jax.numpy as jnp
        import numpy as np
        E, K, D = (8, 2, 128)
        B, S = (2, 512)

        def _layernorm(x, g, b, eps=1e-06):
            m = jnp.mean(x, axis=-1, keepdims=True)
            v = jnp.var(x, axis=-1, keepdims=True)
            return (x - m) * jax.lax.rsqrt(v + eps) * g + b
        orig_shape = x.shape
        xt = x.reshape(-1, orig_shape[-1])
        scores = xt @ gate_w
        ew, ei = jax.lax.top_k(scores, K)
        ew = jax.nn.softmax(ew, axis=-1)
        mask = ei[None, :, :] == jnp.arange(E)[:, None, None]
        wE = jnp.sum(ew[None, :, :] * mask, axis=-1)
        h = jax.nn.gelu(jnp.einsum('td,edf->etf', xt, w1) + b1[:, None, :], approximate=False)
        o = jnp.einsum('etf,efd->etd', h, w2) + b2[:, None, :]
        y = _layernorm(xt[None, :, :] + o, ln_g[:, None, :], ln_b[:, None, :])
        out = jnp.einsum('et,etd->td', wE, y)
        return out.reshape(orig_shape)
    x = L0_attn_x
    mod = (_silu(L0_c) @ L0_wmod).reshape(L0_c.shape[0], 6, 1, -1)
    sa, ca, ga, sb, cb, gb = (mod[:, 0], mod[:, 1], mod[:, 2], mod[:, 3], mod[:, 4], mod[:, 5])
    ga = (2 * (ga >= 0) - 1) * jnp.maximum(jnp.abs(ga), 0.25)
    gb = (2 * (gb >= 0) - 1) * jnp.maximum(jnp.abs(gb), 0.25)
    h = _layernorm(x, axis=-1) * (1 + ca) + sa
    x = x + ga * _L0_attn_ref(h, L0_attn_q_w, L0_attn_q_b, L0_attn_k_w, L0_attn_k_b, L0_attn_v_w, L0_attn_v_b, L0_attn_o_w, L0_attn_o_b)
    h = _layernorm(x, axis=-1) * (1 + cb) + sb
    x = x + gb * _L0_ffn_ref(h, L0_ffn_gate_w, L0_ffn_w1, L0_ffn_b1, L0_ffn_w2, L0_ffn_b2, L0_ffn_ln_g, L0_ffn_ln_b)
    return x

_drawn_inputs = setup_inputs


def setup_inputs(seed=0):
    import zlib

    import numpy as np

    out = dict(_drawn_inputs(seed))
    spreads = {'L0_ffn_b1': (0.0, 0.8),
     'L0_ffn_b2': (0.0, 1.812),
     'L0_ffn_ln_g': (1.0, 0.2),
     'L0_ffn_ln_b': (0.0, 0.454)}
    factors = {'L0_attn_q_w': 8.0,
     'L0_attn_q_b': 8.0,
     'L0_attn_k_w': 8.0,
     'L0_attn_k_b': 64.0,
     'L0_attn_v_w': 8.0,
     'L0_attn_v_b': 8.0,
     'L0_attn_o_w': 8.0,
     'L0_attn_o_b': 8.0,
     'L0_ffn_w1': 8.0,
     'L0_ffn_w2': 7.571}
    for name, (base, spread) in spreads.items():
        noise = np.random.default_rng([zlib.crc32(name.encode()), seed]).standard_normal(out[name].shape)
        drawn = base * np.exp(spread * noise) if base else spread * noise
        out[name] = jnp.asarray(drawn.astype(out[name].dtype))
    for name, factor in factors.items():
        out[name] = (out[name] * factor).astype(out[name].dtype)
    return out
```

```python
import numpy as np
import concourse.bass as bass
from concourse import mybir
from contextlib import ExitStack

BATCH, SEQ, D = 2, 1024, 128
HEADS, DH, WINDOW = 16, 8, 32
EXPERTS, FF = 8, 256
P = 128
STEP = 256
TILES = STEP // P
STEPS = BATCH * SEQ // STEP
PER_BATCH = SEQ // STEP
BLK = WINDOW
KEYS = 2 * BLK
NBLK = STEP // BLK
GROUPS, HG = 4, 4
GC = HG * DH
SPAN = BLK + STEP
QUARTERS = 4
UNITS = 2 * GROUPS
CH = FF // P
HALF = EXPERTS // 2
VP = 3 * DH + 1
LN1_EPS, LN2_EPS, FFN_EPS = 1e-5, 1e-5, 1e-6


def build(nc, t, out):
    fp32, f32r = mybir.dt.float32, mybir.dt.float32r
    bf16, fp16, u32 = mybir.dt.bfloat16, mybir.dt.float16, mybir.dt.uint32
    ALU = mybir.AluOpType
    ACT = mybir.ActivationFunctionType
    AX = mybir.AxisListType.X

    ctx = ExitStack()
    with ctx:
        def sb(name, shape, dt=fp32):
            return ctx.enter_context(nc.sbuf_tensor(name, shape, dt))

        def sem(name):
            return ctx.enter_context(nc.semaphore(name))

        X = sb("x_tokens", [P, STEPS * TILES, D])
        w_qk = sb("w_qk", [P, 2, GROUPS, 3 * GC])
        w_qk_hi = sb("w_qk_hi", [P, 2, GROUPS, 3 * GC], f32r)
        w_qk_lo = sb("w_qk_lo", [P, 2, GROUPS, 3 * GC], f32r)
        b_qk = sb("b_qk", [3 * GC, 2, GROUPS])
        w_v = sb("w_v", [P, D])
        b_v = sb("b_v", [P, 1])
        w_o = sb("w_o", [P, D])
        b_o = sb("b_o", [1, D])
        w_gate = sb("w_gate", [P, EXPERTS])
        w_mod = sb("w_mod", [P, 6, D])
        cT = sb("cT", [P, BATCH])
        w1 = sb("w1", [P, EXPERTS, CH, P])
        w1_hi = sb("w1_hi", [P, EXPERTS, CH, P], f32r)
        w1_lo = sb("w1_lo", [P, EXPERTS, CH, P], f32r)
        b1 = sb("b1", [P, EXPERTS, CH])
        w2 = sb("w2", [P, EXPERTS * CH, D])
        w2_mean = sb("w2_mean", [P, EXPERTS * CH])
        b2 = sb("b2", [1, EXPERTS, D])
        b2_mean = sb("b2_mean", [1, EXPERTS])
        b2_rows = sb("b2_rows", [2, EXPERTS, D], f32r)
        b2_low = sb("b2_low", [1, EXPERTS, D], f32r)
        ln_g = sb("ln_g", [P, EXPERTS, D])
        ln_b = sb("ln_b", [EXPERTS, D])
        ident = sb("ident", [P, P])
        ident16 = sb("ident16", [P, P], fp16)
        center = sb("center", [P, D])
        center_r = sb("center_r", [P, D], f32r)
        rep = sb("rep", [BLK, P])
        rep16 = sb("rep16", [BLK, P], bf16)
        maskf = sb("maskf", [BLK, STEPS + 1, 2, KEYS])
        mask16 = sb("mask16", [BLK, STEPS + 1, 2, KEYS], bf16)
        headmask = sb("headmask", [3 * GC, HG])
        iota = sb("iota", [P, EXPERTS])
        ones = sb("ones", [2, P])
        ones_r = sb("ones_r", [2, P], f32r)
        mhalf = sb("mhalf", [P, 8])
        silu = sb("silu", [P, BATCH])
        silu_den = sb("silu_den", [P, BATCH])
        modT = sb("modT", [P, 4, BATCH])
        gates = sb("gates", [P, BATCH, 2, D])
        gate_sign = sb("gate_sign", [P, BATCH, 2, D])
        w_oG = sb("w_oG", [P, BATCH, D])
        b_oG = sb("b_oG", [1, BATCH, D])
        ln_gG = sb("ln_gG", [P, BATCH, EXPERTS, D])
        ln_bG = sb("ln_bG", [EXPERTS, BATCH, D])
        stats = sb("stats", [P, TILES, 6])
        mv1 = sb("mv1", [P, TILES, 2])
        mv2 = sb("mv2", [P, TILES, 2])
        var1 = sb("var1", [P, TILES])
        var2 = sb("var2", [P, TILES])
        rstd1 = sb("rstd1", [P, TILES])
        rstd2 = sb("rstd2", [P, TILES])
        xn1 = sb("xn1", [P, TILES, D])
        xn2 = sb("xn2", [P, TILES, D])
        hT = sb("hT", [P, SPAN])
        hT_hi = sb("hT_hi", [P, SPAN], f32r)
        hT_lo = sb("hT_lo", [P, SPAN], f32r)
        k_raw = sb("k_raw", [3 * GC, GROUPS, SPAN])
        q_raw = sb("q_raw", [3 * GC, GROUPS, STEP])
        k_st = sb("k_st", [3 * GC, GROUPS, SPAN], f32r)
        q_hl = sb("q_hl", [3 * GC, GROUPS, STEP], f32r)
        q_st = sb("q_st", [3 * GC, GROUPS, NBLK, HG, BLK], f32r)
        v_rest = sb("v_rest", [P, 4 * D])
        v_parts = sb("v_parts", [P, NBLK, HEADS, VP], bf16)
        smax = sb("smax", [P, 2, UNITS])
        sdif = sb("sdif", [P, 2, UNITS * KEYS])
        prob = sb("prob", [P, 2, UNITS * KEYS])
        prob_hl = sb("prob_hl", [P, 2, UNITS, 2, KEYS], fp16)
        probT = sb("probT", [P, 2, UNITS * P], fp16)
        rden = sb("rden", [P, UNITS])
        num = sb("num", [P, UNITS, DH])
        attn = sb("attn", [P, NBLK * GROUPS, DH])
        attnT = sb("attnT", [P, STEP])
        attnTb = sb("attnTb", [P, STEP])
        h2T = sb("h2T", [P, STEP])
        h2_hi = sb("h2_hi", [P, STEP], f32r)
        h2_lo = sb("h2_lo", [P, STEP], f32r)
        gsc = sb("gsc", [P, TILES, EXPERTS])
        gtop = sb("gtop", [P, TILES, 8])
        gidx = sb("gidx", [P, TILES, 8], u32)
        gidf = sb("gidf", [P, TILES, 2])
        gdif = sb("gdif", [P, TILES])
        gexp = sb("gexp", [P, TILES])
        gden = sb("gden", [P, TILES])
        gw = sb("gw", [P, TILES, 2])
        wsel = sb("wsel", [P, TILES, 2, EXPERTS])
        wexp = sb("wexp", [P, TILES, EXPERTS])
        wexpT = sb("wexpT", [EXPERTS, STEP])
        hid = sb("hid", [P, EXPERTS, CH, STEP])
        zsq = sb("zsq", [P, 2, HALF * D])
        zss = sb("zss", [P, 2, HALF])
        zvar = sb("zvar", [P, 2, HALF])
        zrstd = sb("zrstd", [P, 2, HALF])
        zcoef = sb("zcoef", [P, 2, HALF])
        ypart = sb("ypart", [P, TILES, EXPERTS, D])
        ysum = sb("ysum", [P, TILES, D])
        yout = sb("yout", [P, TILES, D])

        def bank(name, shape=(P, 512), dt=fp32):
            return ctx.enter_context(nc.psum_tensor(name, list(shape), dt))

        scoreB = [bank("score0"), bank("score1")]
        probTB = bank("probT_bank", (P, 1024), fp16)
        upB = [bank("up0"), bank("up1")]
        zB = [bank("z0"), bank("z1")]
        M = bank("misc")

        loaded_x, loaded_w, loaded_f = sem("loaded_x"), sem("loaded_w"), sem("loaded_f")
        b2_low_moved = sem("b2_low_moved")
        v_chain, p_chain = sem("v_chain"), sem("p_chain")
        set_pool, set_act, set_pe = sem("set_pool"), sem("set_act"), sem("set_pe")
        set_vec, set_b2 = sem("set_vec"), sem("set_b2")
        stats1, rstd1_s, xn1_s, xT_s, hT_s = sem("stats1"), sem("rstd1_s"), sem("xn1_s"), sem("xT_s"), sem("hT_s")
        kq_proj, kq_raw = sem("kq_proj"), sem("kq_raw")
        k_hi_s, k_ready = sem("k_hi_s"), sem("k_ready")
        q_hi_s, q_lo_s, q_vec, q_pool = sem("q_hi_s"), sem("q_lo_s"), sem("q_vec"), sem("q_pool")
        v_proj, v_out, v_ready = sem("v_proj"), sem("v_out"), sem("v_ready")
        scored, shifted, exped, p_ready = sem("scored"), sem("shifted"), sem("exped"), sem("p_ready")
        p_turned, p_out, pv_done, pv_out = sem("p_turned"), sem("p_out"), sem("pv_done"), sem("pv_out")
        attn_ready, o_done, x1_s = sem("attn_ready"), sem("o_done"), sem("x1_s")
        stats2, rstd2_s, xn2_s, x2T_s, h2_s = sem("stats2"), sem("rstd2_s"), sem("xn2_s"), sem("x2T_s"), sem("h2_s")
        gate_done, gdif_s, gexp_s, wexp_s = sem("gate_done"), sem("gdif_s"), sem("gexp_s"), sem("wexp_s")
        wT_done, wT_out, lnb_done, lnb_out = sem("wT_done"), sem("wT_out"), sem("lnb_done"), sem("lnb_out")
        up_done, gelu_s, z_done, sq_s = sem("up_done"), sem("gelu_s"), sem("z_done"), sem("sq_s")
        ss_s, coef_s, u_done, y_s = sem("ss_s"), sem("coef_s"), sem("u_done"), sem("y_s")
        stored = sem("stored")
        vf_chain, pf_chain = sem("vf_chain"), sem("pf_chain")
        set_ffn, set_att, silu_s, g_out = sem("set_ffn"), sem("set_att"), sem("silu_s"), sem("g_out")
        CH_P = 8

        block = ctx.enter_context(nc.Block())

        def bc(ap, dim, n):
            return ap.unsqueeze(dim).to_broadcast([*ap.shape[:dim], n, *ap.shape[dim:]])

        def blocks(ap):
            return ap.rearrange("p g (b q) -> p g b q", q=BLK)

        def steps(eng, body, between=None):
            body(0, True, False)
            if between:
                between()
            for i in range(1, STEPS):
                body(i, True, True)
            body(STEPS, False, True)

        W_LOADS = [(w_qk, "w_qk"), (b_qk, "b_qk"), (w_v, "w_v"), (b_v, "b_v"), (w_o, "w_o"), (b_o, "b_o"),
                   (w_mod, "w_mod"), (cT, "cT"), (ident, "ident"), (rep, "rep"), (maskf, "masks"),
                   (headmask, "headmask"), (iota, "iota"), (center, "center")]
        F_LOADS = [(w_gate, "w_gate"), (w1, "w1"), (b1, "b1"), (w2, "w2"), (b2, "b2"), (ln_b, "ln_b")]
        x_view = t["x"].rearrange("b (n p) d -> p (b n) d", p=P)
        out_view = out.rearrange("b (n p) d -> p (b n) d", p=P)

        def whole(a):
            return a[tuple(slice(None) for _ in a.shape)]

        @block.sync
        def _(sp):
            for n in range(2):
                h = STEPS * TILES // 2
                sp.dma_start(X[:, n * h:(n + 1) * h, :], x_view[:, n * h:(n + 1) * h, :]).then_inc(loaded_x, 16)
                if n == 0:
                    for dst, name in W_LOADS:
                        sp.dma_start(whole(dst), t[name]).then_inc(loaded_w, 16)
            for dst, name in F_LOADS:
                sp.dma_start(whole(dst), t[name]).then_inc(loaded_f, 16)
            sp.dma_start(ln_g[:, :, :], t["ln_g"].rearrange("e d -> (e d)").partition_broadcast(P)
                         .rearrange("p (e d) -> p e d", e=EXPERTS)).then_inc(loaded_f, 16)
            sp.wait_ge(set_b2, 1)
            sp.dma_start(b2_rows[1:2, :, :].bitcast(fp32), b2_low[:, :, :].bitcast(fp32)).then_inc(b2_low_moved, 16)
            for f in range(STEPS):
                sp.wait_ge(y_s, f + 1)
                sp.dma_start(out_view[:, bass.ds(TILES * f, TILES), :], yout[:, :, :]).then_inc(stored, 16)
            sp.wait_ge(stored, 16 * STEPS)

        @block.gpsimd
        def _(pool):
            g = nc.gpsimd
            g.memset(mhalf[:, :], -0.5)
            g.memset(ones[:, :], 1.0)
            g.memset(v_parts[:, :, :, VP - 1:VP], 1.0)
            g.memset(hT[:, STEP:SPAN], 0.0).then_inc(set_pool, 1)
            pool.wait_ge(set_pool, 1)

            def body(i, att, ffn):
                if att:
                    pool.wait_ge(stats1, i + 1)
                    g.tensor_scalar(var1[:, :], mv1[:, :, 1], LN1_EPS, None, ALU.add).then_inc(p_chain, 1)
                    pool.wait_ge(p_chain, CH_P * i + 1)
                    g.tensor_tensor(rstd1[:, :], var1[:, :], mhalf[:, 0:TILES], ALU.pow).then_inc(rstd1_s, 1)
                    for j in range(2):
                        pool.wait_ge(kq_raw, 6 * i + 2 * j + 2)
                        if j == 0:
                            if i > 0:
                                pool.wait_ge(scored, 4 * i)
                        g.tensor_scalar(k_st[:, 2 * j:2 * j + 2, :], k_raw[:, 2 * j:2 * j + 2, :], 1.0, None,
                                        ALU.mult).then_inc(k_hi_s, 1)
                    for j in range(2):
                        pool.wait_ge(kq_raw, 6 * i + 5 + j)
                        if j == 0:
                            if i > 0:
                                pool.wait_ge(q_vec, 2 * i)
                        g.tensor_scalar(q_hl[:, 2 * j:2 * j + 2, :], q_raw[:, 2 * j:2 * j + 2, :], 1.0, None,
                                        ALU.mult).then_inc(q_hi_s, 1)
                    for j in range(2):
                        pool.wait_ge(q_lo_s, 2 * i + j + 1)
                        for h in range(2, HG):
                            last = g.tensor_scalar(q_st[:, 2 * j:2 * j + 2, :, h, :],
                                                   blocks(q_hl[:, 2 * j:2 * j + 2, :].bitcast(fp32)),
                                                   headmask[:, h:h + 1], None, ALU.mult)
                        last.then_inc(q_pool, 1)
                    for j in range(2):
                        pool.wait_ge(v_out, 2 * i + j + 1)
                        vp = v_parts[:, 4 * j:4 * j + 4, :, :].rearrange("p b h v -> p (b h) v")
                        vr = v_rest[:, :].rearrange("p (n d) -> p n d", d=DH)
                        g.tensor_scalar(vp[:, :, DH:2 * DH], vr, 1.0, None, ALU.mult).then_inc(p_chain, 1)
                        pool.wait_ge(p_chain, CH_P * i + 2 + j)
                        g.tensor_tensor(vp[:, :, 2 * DH:3 * DH], vr, vp[:, :, DH:2 * DH],
                                        ALU.subtract).then_inc(v_ready, 1)

                def split_prob(s):
                    pool.wait_ge(exped, 4 * i + s + 1)
                    if 4 * i + s - 1 > 0:
                        pool.wait_ge(p_turned, 4 * i + s - 1)
                    pr = prob[:, s % 2, :].rearrange("p (u k) -> p u k", k=KEYS)
                    g.tensor_scalar(prob_hl[:, s % 2, :, 0, :], pr, 1.0, None, ALU.mult).then_inc(p_chain, 1)
                    pool.wait_ge(p_chain, CH_P * i + 4 + s)
                    g.tensor_tensor(prob_hl[:, s % 2, :, 1, :], pr, prob_hl[:, s % 2, :, 0, :],
                                    ALU.subtract).then_inc(p_ready, 1)

                def coefficients(f, q):
                    half, tt, b = q // 2, q % 2, q % 2
                    pool.wait_ge(ss_s, 4 * f + q + 1)
                    g.tensor_scalar(zvar[:, b, :], zss[:, b, :], 1.0 / D, FFN_EPS, ALU.mult, ALU.add).then_inc(pf_chain, 1)
                    pool.wait_ge(pf_chain, 8 * f + 2 * q + 1)
                    g.tensor_tensor(zrstd[:, b, :], zvar[:, b, :], mhalf[:, 0:HALF], ALU.pow).then_inc(pf_chain, 1)
                    pool.wait_ge(pf_chain, 8 * f + 2 * q + 2)
                    pool.wait_ge(wexp_s, f + 1)
                    g.tensor_tensor(zcoef[:, b, :], zrstd[:, b, :], wexp[:, tt, half * HALF:(half + 1) * HALF],
                                    ALU.mult).then_inc(coef_s, 1)

                if att:
                    split_prob(0)
                    split_prob(1)
                if ffn:
                    coefficients(i - 1, 0)
                if att:
                    split_prob(2)
                if ffn:
                    coefficients(i - 1, 1)
                if att:
                    split_prob(3)
                if ffn:
                    coefficients(i - 1, 2)
                    coefficients(i - 1, 3)
                if att:
                    pool.wait_ge(stats2, i + 1)
                    g.tensor_scalar(var2[:, :], mv2[:, :, 1], LN2_EPS, None, ALU.add).then_inc(p_chain, 1)
                    pool.wait_ge(p_chain, CH_P * i + 8)
                    g.tensor_tensor(rstd2[:, :], var2[:, :], mhalf[:, 0:TILES], ALU.pow).then_inc(rstd2_s, 1)

            steps(pool, body)

        @block.scalar
        def _(act):
            a = nc.scalar
            act.wait_ge(loaded_w, 16 * len(W_LOADS))
            a.activation(silu_den[:, :], cT[:, :], ACT.Exp, scale=-1.0).then_inc(set_act, 1)
            act.wait_ge(loaded_f, 16 * (len(F_LOADS) + 1))

            def body(i, att, ffn):
                f = i - 1

                def raw_k(g):
                    act.wait_ge(kq_proj, 6 * i + g + 1)
                    if g == 0:
                        if i > 0:
                            act.wait_ge(k_ready, 2 * i)
                    a.activation(k_raw[:, g, :], M[0:3 * GC, 0:SPAN], ACT.Identity,
                                 bias=b_qk[:, 1, g:g + 1]).then_inc(kq_raw, 1)

                def raw_q(j):
                    act.wait_ge(kq_proj, 6 * i + 4 + j + 1)
                    if j == 0:
                        if i > 0:
                            act.wait_ge(q_lo_s, 2 * i)
                    for g in (2 * j, 2 * j + 1):
                        last = a.activation(q_raw[:, g, :], M[0:3 * GC, (g % 2) * STEP:(g % 2 + 1) * STEP],
                                            ACT.Identity, bias=b_qk[:, 0, g:g + 1])
                    last.then_inc(kq_raw, 1)

                def gelu(e):
                    act.wait_ge(up_done, 8 * f + e + 1)
                    if e == 0:
                        if f > 0:
                            act.wait_ge(z_done, 4 * f)
                    for c in range(CH):
                        last = a.activation(hid[:, e, c, :], upB[e % 2][:, c * STEP:(c + 1) * STEP], ACT.Gelu,
                                            bias=b1[:, e, c:c + 1])
                    last.then_inc(gelu_s, 1)

                def exp(s):
                    act.wait_ge(shifted, 4 * i + s + 1)
                    if 4 * i + s - 1 > 0:
                        act.wait_ge(p_ready, 4 * i + s - 1)
                    a.activation(prob[:, s % 2, :], sdif[:, s % 2, :], ACT.Exp,
                                 scale=float(DH) ** -0.5).then_inc(exped, 1)

                def square(q):
                    act.wait_ge(z_done, 4 * f + q + 1)
                    a.activation(zsq[:, q % 2, :], zB[q % 2][:, :], ACT.Square).then_inc(sq_s, 1)

                def take_probT(s):
                    act.wait_ge(p_turned, 4 * i + s + 1)
                    if 4 * i + s - 1 > 0:
                        act.wait_ge(pv_done, 4 * i + s - 1)
                    a.activation(probT[:, s % 2, :], probTB[:, :], ACT.Copy).then_inc(p_out, 1)

                if ffn:
                    for e in range(3):
                        gelu(e)
                for n in range(4):
                    if att:
                        raw_k(n)
                    if ffn:
                        gelu(3 + n)
                if att:
                    raw_q(0)
                if ffn:
                    gelu(7)
                if att:
                    raw_q(1)
                    exp(0)
                    exp(1)
                if ffn:
                    square(0)
                if att:
                    take_probT(0)
                    exp(2)
                if ffn:
                    square(1)
                if att:
                    take_probT(1)
                    exp(3)
                if ffn:
                    square(2)
                if att:
                    take_probT(2)
                if ffn:
                    square(3)
                if att:
                    take_probT(3)
                    act.wait_ge(gdif_s, i + 1)
                    a.activation(gexp[:, :], gdif[:, :], ACT.Exp).then_inc(gexp_s, 1)

            steps(act, body)

        class Chain:

            def __init__(self, eng, s, links):
                self.eng, self.s, self.links, self.n, self.base = eng, s, links, 0, 0

            def start(self, step):
                self.base, self.n = step * self.links, 0

            def link(self, ins):
                self.n += 1
                ins.then_inc(self.s, 1)
                self.eng.wait_ge(self.s, self.base + self.n)

            def end(self):
                assert self.n == self.links, (self.n, self.links)

        @block.vector
        def _(dve):
            v = nc.vector
            pre = Chain(dve, set_vec, 0)

            def split(hi, lo, src):
                pre.link(v.tensor_copy(hi, src))
                return v.tensor_tensor(lo, src, hi.bitcast(fp32), ALU.subtract)

            dve.wait_ge(loaded_w, 16 * len(W_LOADS))
            dve.wait_ge(set_act, 1)
            pre.link(v.tensor_scalar(silu_den[:, :], silu_den[:, :], 1.0, None, ALU.add))
            pre.link(v.reciprocal(silu_den[:, :], silu_den[:, :]))
            v.tensor_tensor(silu[:, :], cT[:, :], silu_den[:, :], ALU.mult).then_inc(silu_s, 1)
            v.tensor_copy(rep16[:, :], rep[:, :])
            v.tensor_copy(mask16[:, :, :, :], maskf[:, :, :, :])
            v.tensor_copy(ident16[:, :], ident[:, :])
            pre.link(split(w_qk_hi[:, :, :, :], w_qk_lo[:, :, :, :], w_qk[:, :, :, :]))
            dve.wait_ge(set_pe, 2)
            mod_ps = M[:, 0:4 * BATCH].rearrange("p (j b) -> p j b", b=BATCH)
            v.tensor_scalar(modT[:, 0:4:2, :], mod_ps[:, 0:4:2, :], 0.0, None, ALU.add)
            v.tensor_scalar(modT[:, 1:4:2, :], mod_ps[:, 1:4:2, :], 1.0, None, ALU.add)
            gate_ps = zB[0][:, :].rearrange("p (b k d) -> p b k d", b=BATCH, k=2)
            v.tensor_scalar(gate_sign[:, :, :, :], gate_ps, 0.0, 2.0, ALU.is_ge, ALU.mult)
            pre.link(v.tensor_scalar(gates[:, :, :, :], gate_ps, -1.0, 0.25, ALU.mult, ALU.max))
            pre.link(v.tensor_tensor(gates[:, :, :, :], gate_ps, gates[:, :, :, :], ALU.max))
            flat = "p b k d -> p (b k d)"
            pre.link(v.scalar_tensor_tensor(gates[:, :, :, :].rearrange(flat), gate_sign[:, :, :, :].rearrange(flat),
                                            -1.0, gates[:, :, :, :].rearrange(flat), ALU.add, ALU.mult))
            v.tensor_tensor(w_oG[:, :, :], bc(w_o[:, :], 1, BATCH), gates[:, :, 0, :], ALU.mult)
            v.tensor_tensor(b_oG[:, :, :], bc(b_o[:, :], 1, BATCH), gates[0:1, :, 0, :],
                            ALU.mult).then_inc(set_att, 1)

            def setup_ffn():
                dve.wait_ge(loaded_f, 16 * (len(F_LOADS) + 1))
                split(w1_hi[:, :, :, :], w1_lo[:, :, :, :], w1[:, :, :, :])
                v.tensor_copy(ones_r[:, :], ones[:, :])
                v.tensor_copy(center_r[:, :], center[:, :])
                v.reduce_sum(w2_mean[:, :], w2[:, :, :], axis=AX)
                pre.link(v.reduce_sum(b2_mean[:, :], b2[:, :, :], axis=AX))
                v.tensor_scalar(w2_mean[:, :], w2_mean[:, :], 1.0 / D, None, ALU.mult)
                pre.link(v.tensor_scalar(b2_mean[:, :], b2_mean[:, :], 1.0 / D, None, ALU.mult))
                v.tensor_tensor(w2[:, :, :], w2[:, :, :], bc(w2_mean[:, :], 2, D), ALU.subtract)
                pre.link(v.tensor_tensor(b2[:, :, :], b2[:, :, :], bc(b2_mean[:, :], 2, D), ALU.subtract))
                split(b2_rows[0:1, :, :], b2_low[:, :, :], b2[:, :, :]).then_inc(set_b2, 1)
                for b in range(BATCH):
                    v.tensor_tensor(ln_gG[:, b, :, :], ln_g[:, :, :], bc(gates[:, b, 1, :], 1, EXPERTS), ALU.mult)
                v.tensor_tensor(ln_bG[:, :, :], bc(ln_b[:, :], 1, BATCH), gates[0:EXPERTS, :, 1, :],
                                ALU.mult).then_inc(set_ffn, 1)
                dve.wait_ge(set_ffn, 1)

            ca, cf = Chain(dve, v_chain, 21), Chain(dve, vf_chain, 6)

            def norm_stats(at, mv):
                for tt in range(TILES):
                    last = v.bn_stats(stats[:, tt, :], X[:, bass.ds(at + tt, 1), :].rearrange("p a d -> p (a d)"))
                ca.link(last)
                for tt in range(TILES):
                    last = v.bn_aggr(mv[:, tt, :], stats[:, tt, :])
                return last

            def normed(dst, at, mv, rstd):
                for tt in range(TILES):
                    last = v.tensor_scalar(dst[:, tt, :], X[:, bass.ds(at + tt, 1), :].rearrange("p a d -> p (a d)"),
                                           mv[:, tt, 0:1], rstd[:, tt:tt + 1], ALU.subtract, ALU.mult)
                return last

            def body(i, att, ffn):
                f = i - 1
                bf = f // PER_BATCH if ffn else None
                b = i // PER_BATCH if att else None
                if att:
                    ca.start(i)
                    if isinstance(i, int):
                        dve.wait_ge(loaded_x, 32)
                    norm_stats(TILES * i, mv1).then_inc(stats1, 1)
                if ffn:
                    cf.start(f)
                    dve.wait_ge(gexp_s, f + 1)
                    cf.link(v.tensor_scalar(gden[:, :], gexp[:, :], 1.0, None, ALU.add))
                    cf.link(v.reciprocal(gw[:, :, 0], gden[:, :]))
                    cf.link(v.tensor_tensor(gw[:, :, 1], gexp[:, :], gw[:, :, 0], ALU.mult))
                    for tt in range(TILES):
                        for j in range(2):
                            last = v.tensor_scalar(wsel[:, tt, j, :], iota[:, :], gidf[:, tt, j:j + 1],
                                                   gw[:, tt, j:j + 1], ALU.is_equal, ALU.mult)
                    cf.link(last)
                    if f > 0:
                        dve.wait_ge(coef_s, 4 * f)
                    if f > 0:
                        dve.wait_ge(wT_done, f)
                    v.tensor_tensor(wexp[:, :, :], wsel[:, :, 0, :], wsel[:, :, 1, :], ALU.add).then_inc(wexp_s, 1)
                if att:
                    dve.wait_ge(rstd1_s, i + 1)
                    if i > 0:
                        dve.wait_ge(xT_s, i)
                    normed(xn1, TILES * i, mv1, rstd1).then_inc(xn1_s, 1)
                if ffn:
                    dve.wait_ge(wT_done, f + 1)
                    if f > 0:
                        dve.wait_ge(lnb_done, f)
                    v.tensor_copy(wexpT[:, :], M[0:EXPERTS, 0:STEP]).then_inc(wT_out, 1)
                    dve.wait_ge(lnb_done, f + 1)
                    xs = X[:, bass.ds(TILES * f, TILES), :]
                    v.tensor_tensor(xs, xs, M[:, 0:STEP].rearrange("p (a d) -> p a d", d=D),
                                    ALU.add).then_inc(lnb_out, 1)
                if att:
                    if i > 0:
                        dve.wait_ge(v_proj, 2 * i)
                    if isinstance(i, int):
                        dve.wait_ge(set_pool, 1)
                    ca.link(v.tensor_copy(hT[:, 0:BLK], hT[:, STEP:SPAN]))
                    dve.wait_ge(xT_s, i + 1)
                    ca.link(v.tensor_scalar(hT[:, BLK:SPAN], M[:, 0:STEP], modT[:, 1, bass.ds(b, 1)],
                                            modT[:, 0, bass.ds(b, 1)], ALU.mult, ALU.add))
                    if i > 0:
                        dve.wait_ge(kq_proj, 6 * i)
                    ca.link(v.tensor_copy(hT_hi[:, :], hT[:, :]))
                    v.tensor_tensor(hT_lo[:, :], hT[:, :], hT_hi[:, :].bitcast(fp32), ALU.subtract).then_inc(hT_s, 1)
                    lk, lq = slice(2 * GC, 3 * GC), slice(GC, 2 * GC)
                    for j in range(2):
                        gg = slice(2 * j, 2 * j + 2)
                        dve.wait_ge(k_hi_s, 2 * i + j + 1)
                        v.tensor_tensor(k_st[lk, gg, :], k_raw[lk, gg, :], k_st[lk, gg, :].bitcast(fp32),
                                        ALU.subtract).then_inc(k_ready, 1)
                    for j in range(2):
                        gg = slice(2 * j, 2 * j + 2)
                        dve.wait_ge(q_hi_s, 2 * i + j + 1)
                        v.tensor_tensor(q_hl[lq, gg, :], q_raw[lq, gg, :], q_hl[lq, gg, :].bitcast(fp32),
                                        ALU.subtract).then_inc(q_lo_s, 1)
                        dve.wait_ge(q_lo_s, 2 * i + j + 1)
                        for h in range(2):
                            last = v.tensor_scalar(q_st[:, gg, :, h, :], blocks(q_hl[:, gg, :].bitcast(fp32)),
                                                   headmask[:, h:h + 1], None, ALU.mult)
                        last.then_inc(q_vec, 1)
                    for j in range(2):
                        dve.wait_ge(v_proj, 2 * i + j + 1)
                        if j == 0:
                            if i > 0:
                                dve.wait_ge(pv_done, 4 * i)
                        vp = v_parts[:, 4 * j:4 * j + 4, :, 0:DH].rearrange("p b h v -> p (b h) v")
                        vm = M[:, :].rearrange("p (n d) -> p n d", d=DH)
                        ca.link(v.tensor_copy(vp, vm))
                        if 2 * i + j > 0:
                            dve.wait_ge(v_ready, 2 * i + j)
                        v.tensor_tensor(v_rest[:, :].rearrange("p (n d) -> p n d", d=DH), vm, vp,
                                        ALU.subtract).then_inc(v_out, 1)

                def shift(s):
                    dve.wait_ge(scored, 4 * i + s + 1)
                    sc = scoreB[s % 2][:, :].rearrange("p (u k) -> p u k", k=KEYS)
                    ca.link(v.reduce_max(smax[:, s % 2, :], sc, axis=AX))
                    if 4 * i + s - 1 > 0:
                        dve.wait_ge(exped, 4 * i + s - 1)
                    v.tensor_tensor(sdif[:, s % 2, :].rearrange("p (u k) -> p u k", k=KEYS), sc,
                                    bc(smax[:, s % 2, :], 2, KEYS), ALU.subtract).then_inc(shifted, 1)

                def take_pv(s):
                    dve.wait_ge(pv_done, 4 * i + s + 1)
                    pv = M[:, 0:UNITS * VP].rearrange("p (u v) -> p u v", v=VP)
                    v.reciprocal(rden[:, :], pv[:, :, VP - 1])
                    v.tensor_reduce(num[:, :, :], pv[:, :, 0:VP - 1].rearrange("p u (a d) -> p u d a", a=3),
                                    axis=AX, op=ALU.add).then_inc(pv_out, 1)
                    dve.wait_ge(pv_out, 4 * i + s + 1)
                    ca.link(v.tensor_tensor(attn[:, s * UNITS:(s + 1) * UNITS, :], num[:, :, :],
                                            bc(rden[:, :], 2, DH), ALU.mult))

                def zsum(q):
                    dve.wait_ge(sq_s, 4 * f + q + 1)
                    v.reduce_sum(zss[:, q % 2, :], zsq[:, q % 2, :].rearrange("p (e d) -> p e d", d=D),
                                 axis=AX).then_inc(ss_s, 1)

                def scale(q):
                    half, tt = q // 2, q % 2
                    dve.wait_ge(coef_s, 4 * f + q + 1)
                    for e in range(HALF):
                        ee = half * HALF + e
                        last = v.scalar_tensor_tensor(
                            ypart[:, tt, ee, :], zB[q % 2][:, e * D:(e + 1) * D], zcoef[:, q % 2, e:e + 1],
                            ln_gG[:, bass.ds(bf, 1), ee, :].rearrange("p a d -> p (a d)"), ALU.mult, ALU.mult)
                    last.then_inc(u_done, 1)

                def finish(tt):
                    dve.wait_ge(u_done, 4 * f + 3 + tt)
                    cf.link(v.tensor_reduce(ysum[:, tt, :], ypart[:, tt, :, :].rearrange("p e d -> p d e"),
                                            axis=AX, op=ALU.add))
                    if tt == 0:
                        if f > 0:
                            dve.wait_ge(stored, 16 * f)
                        dve.wait_ge(lnb_out, f + 1)
                    return v.tensor_tensor(yout[:, tt, :], ysum[:, tt, :],
                                           X[:, bass.ds(TILES * f + tt, 1), :].rearrange("p a d -> p (a d)"), ALU.add)

                if att:
                    shift(0)
                    shift(1)
                if ffn:
                    zsum(0)
                if att:
                    shift(2)
                if ffn:
                    scale(0)
                if att:
                    take_pv(0)
                if ffn:
                    zsum(1)
                if att:
                    shift(3)
                if ffn:
                    scale(1)
                if att:
                    take_pv(1)
                if ffn:
                    zsum(2)
                    scale(2)
                    finish(0)
                if att:
                    take_pv(2)
                if ffn:
                    zsum(3)
                    scale(3)
                    finish(1).then_inc(y_s, 1)
                    cf.end()
                if att:
                    take_pv(3)
                    ca.link(v.transpose(attnT[:, :], attn[:, :, :].rearrange("p n d -> p (n d)")))
                    if i > 0:
                        dve.wait_ge(o_done, i)
                    v.tensor_scalar(attnTb[:, :], attnT[:, :], b_v[:, :], None, ALU.add).then_inc(attn_ready, 1)
                    dve.wait_ge(o_done, i + 1)
                    xs = X[:, bass.ds(TILES * i, TILES), :]
                    v.tensor_tensor(xs, xs, M[:, 0:STEP].rearrange("p (a d) -> p a d", d=D), ALU.add).then_inc(x1_s, 1)
                    dve.wait_ge(x1_s, i + 1)
                    norm_stats(TILES * i, mv2).then_inc(stats2, 1)
                    dve.wait_ge(rstd2_s, i + 1)
                    if i > 0:
                        dve.wait_ge(x2T_s, i)
                    normed(xn2, TILES * i, mv2, rstd2).then_inc(xn2_s, 1)
                    dve.wait_ge(x2T_s, i + 1)
                    ca.link(v.tensor_scalar(h2T[:, :], M[:, 0:STEP], modT[:, 3, bass.ds(b, 1)],
                                            modT[:, 2, bass.ds(b, 1)], ALU.mult, ALU.add))
                    ca.link(v.tensor_copy(h2_hi[:, :], h2T[:, :]))
                    v.tensor_tensor(h2_lo[:, :], h2T[:, :], h2_hi[:, :].bitcast(fp32), ALU.subtract).then_inc(h2_s, 1)
                    dve.wait_ge(gate_done, i + 1)
                    v.tensor_copy(gsc[:, :, :], M[:, 0:TILES * EXPERTS].rearrange("p (a e) -> p a e", e=EXPERTS)
                                  ).then_inc(g_out, 1)
                    dve.wait_ge(g_out, i + 1)
                    for tt in range(TILES):
                        last = v.max(gtop[:, tt, :], gsc[:, tt, :])
                    ca.link(last)
                    for tt in range(TILES):
                        last = v.max_index(gidx[:, tt, :], gtop[:, tt, :], gsc[:, tt, :])
                    ca.link(last)
                    ca.link(v.tensor_copy(gidf[:, :, :], gidx[:, :, 0:2]))
                    v.tensor_tensor(gdif[:, :], gtop[:, :, 1], gtop[:, :, 0], ALU.subtract).then_inc(gdif_s, 1)
                    ca.end()

            steps(dve, body, setup_ffn)

        @block.tensor
        def _(pe):
            mm, tr = nc.tensor.matmul, nc.tensor.transpose

            def three(outp, a_hi, a_lo, b_hi, b_lo):
                mm(outp, a_hi, b_hi, start=True, stop=False)
                mm(outp, a_hi, b_lo, start=False, stop=False)
                return mm(outp, a_lo, b_hi, start=False, stop=True)

            pe.wait_ge(silu_s, 1)
            for n, j in enumerate((0, 1, 3, 4)):
                last = mm(M[:, n * BATCH:(n + 1) * BATCH], w_mod[:, j, :], silu[:, :], start=True, stop=True)
            last.then_inc(set_pe, 1)
            for b in range(BATCH):
                for n, j in enumerate((2, 5)):
                    at = (2 * b + n) * D
                    last = mm(zB[0][:, at:at + D], silu[:, b:b + 1].to_broadcast([P, P]), w_mod[:, j, :],
                              start=True, stop=True)
            last.then_inc(set_pe, 1)
            pe.wait_ge(set_pool, 1)
            pe.wait_ge(set_att, 1)

            def before_ffn():
                pe.wait_ge(set_ffn, 1)
                pe.wait_ge(b2_low_moved, 16)

            def body(i, att, ffn):
                f = i - 1
                bf = f // PER_BATCH if ffn else None
                b = i // PER_BATCH if att else None

                def up(e):
                    if e == 0:
                        pe.wait_ge(h2_s, f + 1)
                    if 8 * f + e - 1 > 0:
                        pe.wait_ge(gelu_s, 8 * f + e - 1)
                    for c in range(CH):
                        last = three(upB[e % 2][:, c * STEP:(c + 1) * STEP], w1_hi[:, e, c, :], w1_lo[:, e, c, :],
                                     h2_hi[:, :], h2_lo[:, :])
                    last.then_inc(up_done, 1)

                def proj_k(g):
                    if g == 0:
                        pe.wait_ge(hT_s, i + 1)
                    else:
                        pe.wait_ge(kq_raw, 6 * i + g)
                    three(M[0:3 * GC, 0:SPAN], w_qk_hi[:, 1, g, :], w_qk_lo[:, 1, g, :], hT_hi[:, :],
                          hT_lo[:, :]).then_inc(kq_proj, 1)

                def proj_q(j):
                    pe.wait_ge(kq_raw, 6 * i + 4 + j)
                    for g in (2 * j, 2 * j + 1):
                        last = three(M[0:3 * GC, (g % 2) * STEP:(g % 2 + 1) * STEP], w_qk_hi[:, 0, g, :],
                                     w_qk_lo[:, 0, g, :], hT_hi[:, BLK:SPAN], hT_lo[:, BLK:SPAN])
                    last.then_inc(kq_proj, 1)

                def proj_v(j):
                    if j == 0:
                        pe.wait_ge(kq_raw, 6 * i + 6)
                    else:
                        pe.wait_ge(v_out, 2 * i + 1)
                    for n in range(4):
                        at = BLK * (4 * j + n)
                        for r in range(2):
                            last = mm(M[r * KEYS:(r + 1) * KEYS, n * D:(n + 1) * D], hT[:, at:at + KEYS], w_v[:, :],
                                      start=True, stop=True)
                    last.then_inc(v_proj, 1)

                def scores(s):
                    if s == 0:
                        pe.wait_ge(k_ready, 2 * i + 2)
                        pe.wait_ge(q_vec, 2 * i + 2)
                        pe.wait_ge(q_pool, 2 * i + 2)
                    if 4 * i + s - 1 > 0:
                        pe.wait_ge(shifted, 4 * i + s - 1)
                    which = mask16[:, bass.ds(i, 1), :, :].rearrange("j a b k -> j (a b) k") if s == 0 \
                        else mask16[:, STEPS, :, :]
                    bank = scoreB[s % 2]
                    mm(bank[:, :].rearrange("p (b g k) -> p b g k", b=2, g=GROUPS), rep16[:, :],
                       bc(which, 2, GROUPS), start=True, stop=False, skip_group_check=True)
                    for u in range(UNITS):
                        blk, g = 2 * s + u // GROUPS, u % GROUPS
                        last = mm(bank[:, u * KEYS:(u + 1) * KEYS], q_st[:, g, blk, :, :].rearrange("p h q -> p (h q)"),
                                  k_st[:, g, blk * BLK:blk * BLK + KEYS], start=False, stop=u == UNITS - 1,
                                  skip_group_check=True)
                    last.then_inc(scored, 1)

                def turn(s):
                    pe.wait_ge(p_ready, 4 * i + s + 1)
                    if 4 * i + s > 0:
                        pe.wait_ge(p_out, 4 * i + s)
                    for u in range(UNITS):
                        last = tr(probTB[:, u * P:(u + 1) * P],
                                  prob_hl[:, s % 2, u, :, :].rearrange("p a k -> p (a k)"), ident16[:, :])
                    last.then_inc(p_turned, 1)

                def values(s):
                    pe.wait_ge(p_out, 4 * i + s + 1)
                    pe.wait_ge(v_ready, 2 * i + 1 + s // 2)
                    if s:
                        if 4 * i + s > 0:
                            pe.wait_ge(pv_out, 4 * i + s)
                    for u in range(UNITS):
                        blk, g = 2 * s + u // GROUPS, u % GROUPS
                        for h in range(HG):
                            last = mm(M[h * BLK:(h + 1) * BLK, u * VP:(u + 1) * VP],
                                      probT[:, s % 2, u * P + h * BLK:u * P + (h + 1) * BLK],
                                      v_parts[:, blk, HG * g + h, :], start=True, stop=True)
                    last.then_inc(pv_done, 1)

                def down(q):
                    half, tt = q // 2, q % 2
                    pe.wait_ge(gelu_s, 8 * f + HALF * (half + 1))
                    if 4 * f + q - 1 > 0:
                        pe.wait_ge(u_done, 4 * f + q - 1)
                    bank, tok = zB[q % 2], slice(tt * P, (tt + 1) * P)
                    by_e = bank[:, :].rearrange("p (e d) -> p e d", d=D)
                    mm(by_e, h2_hi[:, tok], bc(center_r[:, :], 1, HALF), start=True, stop=False,
                       skip_group_check=True)
                    mm(by_e, h2_lo[:, tok], bc(center_r[:, :], 1, HALF), start=False, stop=False,
                       skip_group_check=True)
                    mm(by_e, ones_r[:, :], b2_rows[:, half * HALF:(half + 1) * HALF, :], start=False, stop=False,
                       skip_group_check=True)
                    for e in range(HALF):
                        ee = half * HALF + e
                        for c in range(CH):
                            last = mm(bank[:, e * D:(e + 1) * D], hid[:, ee, c, tok], w2[:, ee * CH + c, :],
                                      start=False, stop=e == HALF - 1 and c == CH - 1, skip_group_check=True)
                    last.then_inc(z_done, 1)

                if ffn:
                    up(0)
                    up(1)
                    pe.wait_ge(wexp_s, f + 1)
                    for tt in range(TILES):
                        last = tr(M[0:EXPERTS, tt * P:(tt + 1) * P], wexp[:, tt, :], ident[:, :])
                    last.then_inc(wT_done, 1)
                    up(2)
                    pe.wait_ge(wT_out, f + 1)
                    for tt in range(TILES):
                        last = mm(M[:, tt * D:(tt + 1) * D], wexpT[:, tt * P:(tt + 1) * P],
                                  ln_bG[:, bass.ds(bf, 1), :].rearrange("e a d -> e (a d)"), start=True, stop=True)
                    last.then_inc(lnb_done, 1)
                if att:
                    pe.wait_ge(xn1_s, i + 1)
                    if ffn:
                        pe.wait_ge(lnb_out, f + 1)
                    for tt in range(TILES):
                        last = tr(M[:, tt * P:(tt + 1) * P], xn1[:, tt, :], ident[:, :])
                    last.then_inc(xT_s, 1)
                if ffn:
                    up(3)
                for n in range(4):
                    if att:
                        proj_k(n)
                    if ffn:
                        up(4 + n)
                if att:
                    proj_q(0)
                    proj_q(1)
                    proj_v(0)
                    proj_v(1)
                    scores(0)
                for s in range(QUARTERS):
                    if att and s < QUARTERS - 1:
                        scores(s + 1)
                    if att and s > 0:
                        values(s - 1)
                    if ffn:
                        down(s)
                    if att:
                        turn(s)
                if att:
                    values(QUARTERS - 1)
                    pe.wait_ge(attn_ready, i + 1)
                    for tt in range(TILES):
                        o = M[:, tt * D:(tt + 1) * D]
                        mm(o, attnTb[:, tt * P:(tt + 1) * P],
                           w_oG[:, bass.ds(b, 1), :].rearrange("p a d -> p (a d)"), start=True, stop=False)
                        last = mm(o, ones[0:1, :], b_oG[:, bass.ds(b, 1), :].rearrange("p a d -> p (a d)"),
                                  start=False, stop=True)
                    last.then_inc(o_done, 1)
                    pe.wait_ge(xn2_s, i + 1)
                    for tt in range(TILES):
                        last = tr(M[:, tt * P:(tt + 1) * P], xn2[:, tt, :], ident[:, :])
                    last.then_inc(x2T_s, 1)
                    pe.wait_ge(h2_s, i + 1)
                    for tt in range(TILES):
                        last = mm(M[:, tt * EXPERTS:(tt + 1) * EXPERTS], h2T[:, tt * P:(tt + 1) * P], w_gate[:, :],
                                  start=True, stop=True)
                    last.then_inc(gate_done, 1)

            steps(pe, body, before_ffn)


def kernel(**inputs):
    import concourse.bacc as bacc
    from concourse.bass_utils import run_bass_kernel_spmd

    def a(name):
        return np.asarray(inputs["L0_" + name])

    def by_group(w):
        w = w.reshape(w.shape[0], GROUPS, 1, GC)
        return np.broadcast_to(w, (w.shape[0], GROUPS, 3, GC)).reshape(w.shape[0], GROUPS, 3 * GC)

    order = np.arange(D).reshape(GROUPS, HG, DH).transpose(1, 0, 2).reshape(D)
    w_qk = np.stack([by_group(a("attn_q_w").T), by_group(a("attn_k_w").T)], 1)
    b_qk = np.stack([by_group(a("attn_q_b")[None]), by_group(a("attn_k_b")[None])], 1)[0].transpose(2, 0, 1)
    j, k = np.arange(BLK)[:, None], np.arange(KEYS)[None, :]
    inner = np.where((k > j) & (k <= j + BLK), 0.0, -1e30)
    first = np.where((k > j) & (k <= j + BLK) & (k >= BLK), 0.0, -1e30)
    masks = np.stack([np.stack([first if s % PER_BATCH == 0 and s < STEPS else inner, inner], 1)
                      for s in range(STEPS + 1)], 1)
    f4 = np.float32
    arrays = {
        "x": a("attn_x"), "w_qk": w_qk, "b_qk": b_qk, "w_v": a("attn_v_w").T,
        "b_v": a("attn_v_b")[order][:, None], "w_o": a("attn_o_w").T[order], "b_o": a("attn_o_b")[None],
        "w_mod": a("wmod").reshape(D, 6, D), "cT": a("c").T,
        "ident": np.eye(P, dtype=f4), "rep": np.tile(np.eye(BLK, dtype=f4), (1, HG)), "masks": masks.astype(f4),
        "headmask": (np.arange(3 * GC)[:, None] % GC // DH == np.arange(HG)[None, :]).astype(f4),
        "iota": np.broadcast_to(np.arange(EXPERTS, dtype=f4), (P, EXPERTS)),
        "center": (np.eye(D) - 1.0 / D).astype(f4),
        "w_gate": a("ffn_gate_w"), "w1": a("ffn_w1").reshape(EXPERTS, D, CH, P).transpose(1, 0, 2, 3),
        "b1": a("ffn_b1").reshape(EXPERTS, CH, P).transpose(2, 0, 1),
        "w2": a("ffn_w2").reshape(EXPERTS * CH, P, D).transpose(1, 0, 2), "b2": a("ffn_b2")[None],
        "ln_g": a("ffn_ln_g"), "ln_b": a("ffn_ln_b"),
    }
    arrays = {name: np.ascontiguousarray(x) for name, x in arrays.items()}
    nc = bacc.Bacc("TRN2", target_bir_lowering=False, num_devices=1)
    dram = {name: nc.dram_tensor(f"in_{name}", x.shape, mybir.dt.from_np(x.dtype), kind="ExternalInput").ap()
            for name, x in arrays.items()}
    out = nc.dram_tensor("out_x", (BATCH, SEQ, D), mybir.dt.float32, kind="ExternalOutput").ap()
    build(nc, dram, out)
    r = run_bass_kernel_spmd(nc, [{f"in_{name}": x for name, x in arrays.items()}], core_ids=[0])
    return r.results[0]["out_x"]
```

```python
import numpy as np
import concourse.bass as bass
from concourse import mybir
from contextlib import ExitStack

BATCH, SEQ, D = 2, 1024, 128
HEADS, DH, WINDOW = 16, 8, 32
EXPERTS, FF = 8, 256
P = 128
STEP = 256
TILES = STEP // P
STEPS = BATCH * SEQ // STEP
PER_BATCH = SEQ // STEP
BLK = WINDOW
KEYS = 2 * BLK
NBLK = STEP // BLK
GROUPS, HG = 4, 4
GC = HG * DH
SPAN = BLK + STEP
QUARTERS = 4
UNITS = 2 * GROUPS
CH = FF // P
HALF = EXPERTS // 2
VP = 3 * DH + 1
LN1_EPS, LN2_EPS, FFN_EPS = 1e-5, 1e-5, 1e-6


def build(nc, t, out):
    fp32, f32r = mybir.dt.float32, mybir.dt.float32r
    bf16, fp16, u32 = mybir.dt.bfloat16, mybir.dt.float16, mybir.dt.uint32
    ALU = mybir.AluOpType
    ACT = mybir.ActivationFunctionType
    AX = mybir.AxisListType.X

    ctx = ExitStack()
    with ctx:
        def sb(name, shape, dt=fp32):
            return ctx.enter_context(nc.sbuf_tensor(name, shape, dt))

        def sem(name):
            return ctx.enter_context(nc.semaphore(name))

        X = sb("x_tokens", [P, STEPS * TILES, D])
        w_qk = sb("w_qk", [P, 2, GROUPS, 3 * GC])
        w_qk_hi = sb("w_qk_hi", [P, 2, GROUPS, 3 * GC], f32r)
        w_qk_lo = sb("w_qk_lo", [P, 2, GROUPS, 3 * GC], f32r)
        b_qk = sb("b_qk", [3 * GC, 2, GROUPS])
        w_v = sb("w_v", [P, D])
        b_v = sb("b_v", [P, 1])
        w_o = sb("w_o", [P, D])
        b_o = sb("b_o", [1, D])
        w_gate = sb("w_gate", [P, EXPERTS])
        w_mod = sb("w_mod", [P, 6, D])
        cT = sb("cT", [P, BATCH])
        w1 = sb("w1", [P, EXPERTS, CH, P])
        w1_hi = sb("w1_hi", [P, EXPERTS, CH, P], f32r)
        w1_lo = sb("w1_lo", [P, EXPERTS, CH, P], f32r)
        b1 = sb("b1", [P, EXPERTS, CH])
        w2 = sb("w2", [P, EXPERTS * CH, D])
        w2_mean = sb("w2_mean", [P, EXPERTS * CH])
        b2 = sb("b2", [1, EXPERTS, D])
        b2_mean = sb("b2_mean", [1, EXPERTS])
        b2_rows = sb("b2_rows", [2, EXPERTS, D], f32r)
        b2_low = sb("b2_low", [1, EXPERTS, D], f32r)
        ln_g = sb("ln_g", [P, EXPERTS, D])
        ln_b = sb("ln_b", [EXPERTS, D])
        ident = sb("ident", [P, P])
        ident16 = sb("ident16", [P, P], fp16)
        center = sb("center", [P, D])
        center_r = sb("center_r", [P, D], f32r)
        rep = sb("rep", [BLK, P])
        rep16 = sb("rep16", [BLK, P], bf16)
        maskf = sb("maskf", [BLK, STEPS + 1, 2, KEYS])
        mask16 = sb("mask16", [BLK, STEPS + 1, 2, KEYS], bf16)
        headmask = sb("headmask", [3 * GC, HG])
        iota = sb("iota", [P, EXPERTS])
        ones = sb("ones", [2, P])
        one = sb("one", [P, 1])
        ones_r = sb("ones_r", [2, P], f32r)
        mhalf = sb("mhalf", [P, 8])
        silu = sb("silu", [P, BATCH])
        silu_den = sb("silu_den", [P, BATCH])
        modT = sb("modT", [P, 4, BATCH])
        gates = sb("gates", [P, BATCH, 2, D])
        gate_sign = sb("gate_sign", [P, BATCH, 2, D])
        w_oG = sb("w_oG", [P, BATCH, D])
        b_oG = sb("b_oG", [1, BATCH, D])
        ln_gG = sb("ln_gG", [P, BATCH, EXPERTS, D])
        ln_bG = sb("ln_bG", [EXPERTS, BATCH, D])
        stats = sb("stats", [P, TILES, 6])
        mv1 = sb("mv1", [P, TILES, 2])
        mv2 = sb("mv2", [P, TILES, 2])
        var1 = sb("var1", [P, TILES])
        var2 = sb("var2", [P, TILES])
        rstd1 = sb("rstd1", [P, TILES])
        rstd2 = sb("rstd2", [P, TILES])
        xn1 = sb("xn1", [P, TILES, D])
        xn2 = sb("xn2", [P, TILES, D])
        hT = sb("hT", [P, SPAN])
        hT_hi = sb("hT_hi", [P, SPAN], f32r)
        hT_lo = sb("hT_lo", [P, SPAN], f32r)
        k_st = sb("k_st", [3 * GC, GROUPS, SPAN], f32r)
        q_hl = sb("q_hl", [3 * GC, GROUPS, STEP], f32r)
        q_st = sb("q_st", [3 * GC, GROUPS, NBLK, HG, BLK], f32r)
        v_rest = sb("v_rest", [P, 2, 4 * D])
        v_parts = sb("v_parts", [P, NBLK, HEADS, VP], bf16)
        smax = sb("smax", [P, 2, UNITS])
        sdif = sb("sdif", [P, 2, UNITS * KEYS])
        prob = sb("prob", [P, 2, UNITS * KEYS])
        prob_hl = sb("prob_hl", [P, 2, UNITS, 2, KEYS], fp16)
        probT = sb("probT", [P, 2, UNITS * P], fp16)
        rden = sb("rden", [P, UNITS])
        num = sb("num", [P, UNITS, DH])
        attn = sb("attn", [P, NBLK * GROUPS, DH])
        attnT = sb("attnT", [P, STEP])
        attnTb = sb("attnTb", [P, STEP])
        h2T = sb("h2T", [P, STEP])
        h2_hi = sb("h2_hi", [P, STEP], f32r)
        h2_lo = sb("h2_lo", [P, STEP], f32r)
        gsc = sb("gsc", [P, TILES, EXPERTS])
        gtop = sb("gtop", [P, TILES, 8])
        gidx = sb("gidx", [P, TILES, 8], u32)
        gidf = sb("gidf", [P, TILES, 2])
        gdif = sb("gdif", [P, TILES])
        gexp = sb("gexp", [P, TILES])
        gden = sb("gden", [P, TILES])
        gw = sb("gw", [P, TILES, 2])
        wsel = sb("wsel", [P, TILES, 2, EXPERTS])
        wexp = sb("wexp", [P, TILES, EXPERTS])
        wexpT = sb("wexpT", [EXPERTS, STEP])
        hid = sb("hid", [P, EXPERTS, CH, STEP])
        zsq = sb("zsq", [P, 2, HALF * D])
        zss = sb("zss", [P, 2, HALF])
        zvar = sb("zvar", [P, 2, HALF])
        zrstd = sb("zrstd", [P, 2, HALF])
        zcoef = sb("zcoef", [P, 2, HALF])
        ypart = sb("ypart", [P, TILES, EXPERTS, D])
        yout = sb("yout", [P, TILES, D])

        def bank(name, shape=(P, 512), dt=fp32):
            return ctx.enter_context(nc.psum_tensor(name, list(shape), dt))

        scoreB = [bank("score0"), bank("score1")]
        probTB = bank("probT_bank", (P, 1024), fp16)
        U = [bank("turns0"), bank("turns1")]
        zB = [bank("z0"), bank("z1")]
        M = bank("misc")

        loaded_x, loaded_w, loaded_f = sem("loaded_x"), sem("loaded_w"), sem("loaded_f")
        b2_low_moved = sem("b2_low_moved")
        set_pool, set_act, set_pe = sem("set_pool"), sem("set_act"), sem("set_pe")
        set_vec, set_b2, set_att, silu_s = sem("set_vec"), sem("set_b2"), sem("set_att"), sem("silu_s")
        w1_hi_s, w1_lo_s, w2_s, lng_s, gates_s = sem("w1_hi_s"), sem("w1_lo_s"), sem("w2_s"), sem("lng_s"), sem("gates_s")
        v_front, v_att, v_ffn = sem("v_front"), sem("v_att"), sem("v_ffn")
        p_front, p_att, p_ffn = sem("p_front"), sem("p_att"), sem("p_ffn")
        stats1, rstd1_s, xn1_s, xT_s = sem("stats1"), sem("rstd1_s"), sem("xn1_s"), sem("xT_s")
        hT_hi_s, hT_s = sem("hT_hi_s"), sem("hT_s")
        kq_proj, kq_hi, k_ready = sem("kq_proj"), sem("kq_hi"), sem("k_ready")
        q_lo_s, q_vec, q_pool = sem("q_lo_s"), sem("q_vec"), sem("q_pool")
        v_proj, v_hi_s, v_out, v_ready = sem("v_proj"), sem("v_hi_s"), sem("v_out"), sem("v_ready")
        scored, shifted, exped, p_ready = sem("scored"), sem("shifted"), sem("exped"), sem("p_ready")
        p_turned, p_out, pv_done, pv_out = sem("p_turned"), sem("p_out"), sem("pv_done"), sem("pv_out")
        attn_ready, o_done, x1_s = sem("attn_ready"), sem("o_done"), sem("x1_s")
        stats2, rstd2_s, xn2_s, x2T_s = sem("stats2"), sem("rstd2_s"), sem("xn2_s"), sem("x2T_s")
        h2_s = sem("h2_s")
        gate_done, g_out, gdif_s, gexp_s, wexp_s = sem("gate_done"), sem("g_out"), sem("gdif_s"), sem("gexp_s"), sem("wexp_s")
        wT_done, wT_out, lnb_done, lnb_out = sem("wT_done"), sem("wT_out"), sem("lnb_done"), sem("lnb_out")
        up_done, gelu_s, z_done, sq_s = sem("up_done"), sem("gelu_s"), sem("z_done"), sem("sq_s")
        ss_s, coef_s, u_done, y_s = sem("ss_s"), sem("coef_s"), sem("u_done"), sem("y_s")
        stored = sem("stored")

        block = ctx.enter_context(nc.Block())

        def bc(ap, dim, n):
            return ap.unsqueeze(dim).to_broadcast([*ap.shape[:dim], n, *ap.shape[dim:]])

        def blocks(ap):
            return ap.rearrange("p g (b q) -> p g b q", q=BLK)

        def by_key(ap):
            return ap.rearrange("p (u k) -> p u k", k=KEYS)

        def steps(front, body):
            front(0)
            for i in range(STEPS + 1):
                body(i, i < STEPS, i > 0, i + 1 < STEPS)

        class Chain:

            def __init__(self, eng, s):
                self.eng, self.s, self.n = eng, s, 0

            def link(self, ins):
                self.n += 1
                ins.then_inc(self.s, 1)
                self.eng.wait_ge(self.s, self.n)

        W_LOADS = [(cT, "cT"), (w_mod, "w_mod"), (w_qk, "w_qk"), (ident, "ident"), (b_qk, "b_qk"), (w_v, "w_v"),
                   (b_v, "b_v"), (w_o, "w_o"), (b_o, "b_o"), (rep, "rep"), (maskf, "masks"),
                   (headmask, "headmask"), (iota, "iota"), (center, "center")]
        F_LOADS = [(w1, "w1"), (w_gate, "w_gate"), (b1, "b1"), (w2, "w2"), (b2, "b2"), (ln_b, "ln_b")]
        ALL_W, ALL_F = 16 * len(W_LOADS), 16 * (len(F_LOADS) + 1)
        x_view = t["x"].rearrange("b (n p) d -> p (b n) d", p=P)
        out_view = out.rearrange("b (n p) d -> p (b n) d", p=P)

        def whole(a):
            return a[tuple(slice(None) for _ in a.shape)]

        @block.sync
        def _(sp):
            for dst, name in W_LOADS[:4]:
                sp.dma_start(whole(dst), t[name]).then_inc(loaded_w, 16)
            sp.dma_start(X[:, :, :], x_view).then_inc(loaded_x, 16)
            for dst, name in W_LOADS[4:]:
                sp.dma_start(whole(dst), t[name]).then_inc(loaded_w, 16)
            for dst, name in F_LOADS:
                sp.dma_start(whole(dst), t[name]).then_inc(loaded_f, 16)
            sp.dma_start(ln_g[:, :, :], t["ln_g"].rearrange("e d -> (e d)").partition_broadcast(P)
                         .rearrange("p (e d) -> p e d", e=EXPERTS)).then_inc(loaded_f, 16)
            sp.wait_ge(set_b2, 1)
            sp.dma_start(b2_rows[1:2, :, :].bitcast(fp32), b2_low[:, :, :].bitcast(fp32)).then_inc(b2_low_moved, 16)
            for f in range(STEPS):
                sp.wait_ge(y_s, f + 1)
                sp.dma_start(out_view[:, TILES * f:TILES * (f + 1), :], yout[:, :, :]).then_inc(stored, 16)
            sp.wait_ge(stored, 16 * STEPS)

        @block.gpsimd
        def _(pool):
            g = nc.gpsimd
            cn, ca, cf = Chain(pool, p_front), Chain(pool, p_att), Chain(pool, p_ffn)
            g.memset(mhalf[:, :], -0.5)
            g.memset(one[:, :], 1.0)
            g.memset(ones[:, :], 1.0)
            g.memset(v_parts[:, :, :, VP - 1:VP], 1.0)
            g.memset(hT[:, STEP:SPAN], 0.0).then_inc(set_pool, 1)
            pool.wait_ge(set_pool, 1)

            def rstd_front(n):
                pool.wait_ge(stats1, n + 1)
                cn.link(g.tensor_scalar(var1[:, :], mv1[:, :, 1], LN1_EPS, None, ALU.add))
                g.tensor_tensor(rstd1[:, :], var1[:, :], mhalf[:, 0:TILES], ALU.pow).then_inc(rstd1_s, 1)

            def split_v(n, j):
                pool.wait_ge(v_out, 2 * n + j + 1)
                vp = v_parts[:, 4 * j:4 * j + 4, :, :].rearrange("p b h v -> p (b h) v")
                vr = v_rest[:, j, :].rearrange("p (n d) -> p n d", d=DH)
                cn.link(g.tensor_tensor(vp[:, :, DH:2 * DH], vr, one[:, :].unsqueeze(2).to_broadcast([P, 4 * HEADS, DH]), ALU.mult))
                g.tensor_tensor(vp[:, :, 2 * DH:3 * DH], vr, vp[:, :, DH:2 * DH], ALU.subtract).then_inc(v_ready, 1)

            def mask_q(n, j):
                pool.wait_ge(q_lo_s, 2 * n + j + 1)
                gg, h = slice(2 * j, 2 * j + 2), HG - 1
                keep = headmask[:, h:h + 1].unsqueeze(2).unsqueeze(3).to_broadcast([3 * GC, 2, NBLK, BLK])
                g.tensor_tensor(q_st[:, gg, :, h, :], blocks(q_hl[:, gg, :].bitcast(fp32)), keep,
                                ALU.mult).then_inc(q_pool, 1)

            def low_prob(i, s):
                pool.wait_ge(exped, 4 * i + s + 1)
                g.tensor_tensor(prob_hl[:, s % 2, :, 1, :], by_key(prob[:, s % 2, :]), prob_hl[:, s % 2, :, 0, :],
                                ALU.subtract).then_inc(p_ready, 1)

            def coefficients(f, q):
                half, tt, b = q // 2, q % 2, q % 2
                pool.wait_ge(ss_s, 4 * f + q + 1)
                cf.link(g.tensor_scalar(zvar[:, b, :], zss[:, b, :], 1.0 / D, FFN_EPS, ALU.mult, ALU.add))
                cf.link(g.tensor_tensor(zrstd[:, b, :], zvar[:, b, :], mhalf[:, 0:HALF], ALU.pow))
                pool.wait_ge(wexp_s, f + 1)
                if 4 * f + q - 1 > 0:
                    pool.wait_ge(u_done, 4 * f + q - 1)
                g.tensor_tensor(zcoef[:, b, :], zrstd[:, b, :], wexp[:, tt, half * HALF:(half + 1) * HALF],
                                ALU.mult).then_inc(coef_s, 1)

            def finish(f, tt):
                pool.wait_ge(u_done, 4 * f + 3 + tt)
                for n in (4, 2, 1):
                    cf.link(g.tensor_tensor(ypart[:, tt, 0:n, :], ypart[:, tt, 0:n, :], ypart[:, tt, n:2 * n, :],
                                            ALU.add))
                pool.wait_ge(lnb_out, f + 1)
                if tt == 0:
                    if f > 0:
                        pool.wait_ge(stored, 16 * f)
                last = g.tensor_tensor(yout[:, tt, :], ypart[:, tt, 0, :], X[:, TILES * f + tt, :], ALU.add)
                if tt == 1:
                    last.then_inc(y_s, 1)

            def low_w1(h):
                if h == 0:
                    pool.wait_ge(w1_hi_s, 1)
                ee = slice(h * HALF, (h + 1) * HALF)
                g.tensor_tensor(w1_lo[:, ee, :, :], w1[:, ee, :, :], w1_hi[:, ee, :, :].bitcast(fp32),
                                ALU.subtract).then_inc(w1_lo_s, 1)

            def gated_ln(b):
                if b == 0:
                    pool.wait_ge(gates_s, 1)
                g.tensor_tensor(ln_gG[:, b, :, :], ln_g[:, :, :], bc(gates[:, b, 1, :], 1, EXPERTS), ALU.mult)
                g.tensor_tensor(ln_bG[:, b, :], ln_b[:, :], gates[0:EXPERTS, b, 1, :], ALU.mult).then_inc(lng_s, 1)

            def front(n):
                rstd_front(n)
                split_v(n, 0)
                for j in range(2):
                    mask_q(n, j)
                split_v(n, 1)

            def body(i, att, ffn, nxt):
                n, f = i + 1, i - 1
                if att:
                    low_prob(i, 0)
                if i == 0:
                    low_w1(0)
                if att:
                    low_prob(i, 1)
                if i == 0:
                    low_w1(1)
                if nxt:
                    rstd_front(n)
                if ffn:
                    coefficients(f, 0)
                if att:
                    low_prob(i, 2)
                if i == 0:
                    gated_ln(0)
                if ffn:
                    coefficients(f, 1)
                if att:
                    low_prob(i, 3)
                if i == 0:
                    gated_ln(1)
                if ffn:
                    coefficients(f, 2)
                if nxt:
                    split_v(n, 0)
                if att:
                    pool.wait_ge(stats2, i + 1)
                    ca.link(g.tensor_scalar(var2[:, :], mv2[:, :, 1], LN2_EPS, None, ALU.add))
                    g.tensor_tensor(rstd2[:, :], var2[:, :], mhalf[:, 0:TILES], ALU.pow).then_inc(rstd2_s, 1)
                if ffn:
                    finish(f, 0)
                if nxt:
                    mask_q(n, 0)
                if ffn:
                    coefficients(f, 3)
                if nxt:
                    mask_q(n, 1)
                    split_v(n, 1)
                if ffn:
                    finish(f, 1)

            steps(front, body)

        @block.scalar
        def _(act):
            a = nc.scalar
            act.wait_ge(loaded_w, ALL_W)
            a.activation(silu_den[:, :], cT[:, :], ACT.Exp, scale=-1.0).then_inc(set_act, 1)

            def hi_hT(n):
                act.wait_ge(xT_s, n + 1)
                if n > 0:
                    act.wait_ge(kq_proj, 6 * n)
                b = n // PER_BATCH
                a.activation(hT_hi[:, BLK:SPAN], U[0][:, 0:STEP], ACT.Identity, bias=modT[:, 0, b:b + 1],
                             scale=modT[:, 1, b:b + 1]).then_inc(hT_hi_s, 1)

            def hi_k(n, g):
                act.wait_ge(kq_proj, 6 * n + g + 1)
                if g == 0:
                    if n > 0:
                        act.wait_ge(scored, 4 * n)
                a.activation(k_st[:, g, :], U[(g + 1) % 2][0:3 * GC, 0:SPAN], ACT.Identity,
                             bias=b_qk[:, 1, g:g + 1]).then_inc(kq_hi, 1)

            def hi_q(n, j):
                act.wait_ge(kq_proj, 6 * n + 5 + j)
                if j == 0:
                    if n > 0:
                        act.wait_ge(q_vec, 2 * n)
                    if n > 0:
                        act.wait_ge(q_pool, 2 * n)
                for g in (2 * j, 2 * j + 1):
                    last = a.activation(q_hl[:, g, :], U[j][0:3 * GC, (g % 2) * STEP:(g % 2 + 1) * STEP],
                                        ACT.Identity, bias=b_qk[:, 0, g:g + 1])
                last.then_inc(kq_hi, 1)

            def hi_v(n, j):
                act.wait_ge(v_proj, 2 * n + j + 1)
                if j == 0:
                    if n > 0:
                        act.wait_ge(pv_done, 4 * n)
                a.activation(v_parts[:, 4 * j:4 * j + 4, :, 0:DH].rearrange("p b h v -> p (b h) v"),
                             U[1 - j][:, :].rearrange("p (n d) -> p n d", d=DH), ACT.Copy).then_inc(v_hi_s, 1)

            def exp(i, s):
                act.wait_ge(shifted, 4 * i + s + 1)
                if 4 * i + s - 1 > 0:
                    act.wait_ge(p_turned, 4 * i + s - 1)
                sd = sdif[:, s % 2, :]
                a.activation(prob_hl[:, s % 2, :, 0, :], by_key(sd), ACT.Exp, scale=float(DH) ** -0.5)
                if 4 * i + s - 1 > 0:
                    act.wait_ge(p_ready, 4 * i + s - 1)
                a.activation(prob[:, s % 2, :], sd, ACT.Exp, scale=float(DH) ** -0.5).then_inc(exped, 1)

            def take_probT(i, s):
                act.wait_ge(p_turned, 4 * i + s + 1)
                if 4 * i + s - 1 > 0:
                    act.wait_ge(pv_done, 4 * i + s - 1)
                a.activation(probT[:, s % 2, :], probTB[:, :], ACT.Copy).then_inc(p_out, 1)

            def square(f, q):
                act.wait_ge(z_done, 4 * f + q + 1)
                if 4 * f + q - 1 > 0:
                    act.wait_ge(ss_s, 4 * f + q - 1)
                a.activation(zsq[:, q % 2, :], zB[q % 2][:, :], ACT.Square).then_inc(sq_s, 1)

            def gelu(i, e):
                act.wait_ge(up_done, 8 * i + e + 1)
                if e == 0:
                    if i > 0:
                        act.wait_ge(z_done, 4 * i)
                for c in range(CH):
                    last = a.activation(hid[:, e, c, :], U[(e + 1) % 2][:, c * STEP:(c + 1) * STEP], ACT.Gelu,
                                        bias=b1[:, e, c:c + 1])
                last.then_inc(gelu_s, 1)

            def front(n):
                act.wait_ge(set_att, 1)
                hi_hT(n)
                for g in range(GROUPS):
                    hi_k(n, g)
                hi_v(n, 0)
                hi_q(n, 0)
                hi_q(n, 1)
                hi_v(n, 1)
                act.wait_ge(loaded_f, ALL_F)
                a.activation(w1_hi[:, :, :, :], w1[:, :, :, :], ACT.Copy).then_inc(w1_hi_s, 1)

            def body(i, att, ffn, nxt):
                n, f = i + 1, i - 1
                if ffn:
                    act.wait_ge(gdif_s, f + 1)
                    a.activation(gexp[:, :], gdif[:, :], ACT.Exp).then_inc(gexp_s, 1)
                if att:
                    exp(i, 0)
                    exp(i, 1)
                if ffn:
                    square(f, 0)
                if att:
                    take_probT(i, 0)
                    exp(i, 2)
                if ffn:
                    square(f, 1)
                if nxt:
                    hi_hT(n)
                if att:
                    take_probT(i, 1)
                    exp(i, 3)
                if ffn:
                    square(f, 2)
                if nxt:
                    hi_k(n, 0)
                    hi_k(n, 1)
                if att:
                    take_probT(i, 2)
                if nxt:
                    hi_k(n, 2)
                    hi_k(n, 3)
                if att:
                    take_probT(i, 3)
                if nxt:
                    hi_v(n, 0)
                    hi_q(n, 0)
                if ffn:
                    square(f, 3)
                if nxt:
                    hi_q(n, 1)
                    hi_v(n, 1)
                if att:
                    for e in range(EXPERTS):
                        gelu(i, e)

            steps(front, body)

        @block.vector
        def _(dve):
            v = nc.vector
            pre = Chain(dve, set_vec)
            cn, ca, cf = Chain(dve, v_front), Chain(dve, v_att), Chain(dve, v_ffn)

            def split(hi, lo, src):
                pre.link(v.tensor_copy(hi, src))
                return v.tensor_tensor(lo, src, hi.bitcast(fp32), ALU.subtract)

            def norm_stats(chain, at, mv):
                for tt in range(TILES):
                    last = v.bn_stats(stats[:, tt, :], X[:, at + tt, :])
                chain.link(last)
                for tt in range(TILES):
                    last = v.bn_aggr(mv[:, tt, :], stats[:, tt, :])
                return last

            def normed(dst, at, mv, rstd):
                for tt in range(TILES):
                    last = v.tensor_scalar(dst[:, tt, :], X[:, at + tt, :],
                                           mv[:, tt, 0:1], rstd[:, tt:tt + 1], ALU.subtract, ALU.mult)
                return last

            def stats_front(n):
                dve.wait_ge(loaded_x, 16)
                norm_stats(cn, TILES * n, mv1).then_inc(stats1, 1)

            def normed_front(n):
                dve.wait_ge(rstd1_s, n + 1)
                if n > 0:
                    dve.wait_ge(xT_s, n)
                normed(xn1, TILES * n, mv1, rstd1).then_inc(xn1_s, 1)

            def take_hT(n):
                b = n // PER_BATCH
                if n > 0:
                    dve.wait_ge(v_proj, 2 * n)
                if n == 0:
                    dve.wait_ge(set_pool, 1)
                cn.link(v.tensor_copy(hT[:, 0:BLK], hT[:, STEP:SPAN]))
                dve.wait_ge(hT_hi_s, n + 1)
                v.tensor_scalar(hT[:, BLK:SPAN], U[0][:, 0:STEP], modT[:, 1, b:b + 1],
                                modT[:, 0, b:b + 1], ALU.mult, ALU.add)
                cn.link(v.tensor_copy(hT_hi[:, 0:BLK], hT[:, 0:BLK]))
                v.tensor_tensor(hT_lo[:, :], hT[:, :], hT_hi[:, :].bitcast(fp32), ALU.subtract).then_inc(hT_s, 1)

            lk, lq = slice(2 * GC, 3 * GC), slice(GC, 2 * GC)

            def low_k(n, g):
                dve.wait_ge(kq_hi, 6 * n + g + 1)
                v.scalar_tensor_tensor(k_st[lk, g, :], U[(g + 1) % 2][lk, 0:SPAN], b_qk[lk, 1, g:g + 1],
                                       k_st[lk, g, :].bitcast(fp32), ALU.add, ALU.subtract).then_inc(k_ready, 1)

            def low_q(n, j):
                dve.wait_ge(kq_hi, 6 * n + 5 + j)
                for g in (2 * j, 2 * j + 1):
                    last = v.scalar_tensor_tensor(q_hl[lq, g, :], U[j][lq, (g % 2) * STEP:(g % 2 + 1) * STEP],
                                                  b_qk[lq, 0, g:g + 1], q_hl[lq, g, :].bitcast(fp32),
                                                  ALU.add, ALU.subtract)
                last.then_inc(q_lo_s, 1)

            def mask_q(n, j):
                dve.wait_ge(q_lo_s, 2 * n + j + 1)
                gg = slice(2 * j, 2 * j + 2)
                for h in range(HG - 1):
                    last = v.tensor_scalar(q_st[:, gg, :, h, :], blocks(q_hl[:, gg, :].bitcast(fp32)),
                                           headmask[:, h:h + 1], None, ALU.mult)
                last.then_inc(q_vec, 1)

            def rest_v(n, j):
                dve.wait_ge(v_hi_s, 2 * n + j + 1)
                if 2 * n + j - 1 > 0:
                    dve.wait_ge(v_ready, 2 * n + j - 1)
                v.tensor_tensor(v_rest[:, j, :].rearrange("p (n d) -> p n d", d=DH),
                                U[1 - j][:, :].rearrange("p (n d) -> p n d", d=DH),
                                v_parts[:, 4 * j:4 * j + 4, :, 0:DH].rearrange("p b h v -> p (b h) v"),
                                ALU.subtract).then_inc(v_out, 1)

            def shift(i, s):
                dve.wait_ge(scored, 4 * i + s + 1)
                sc = by_key(scoreB[s % 2][:, :])
                ca.link(v.reduce_max(smax[:, s % 2, :], sc, axis=AX))
                if 4 * i + s - 1 > 0:
                    dve.wait_ge(exped, 4 * i + s - 1)
                v.tensor_tensor(by_key(sdif[:, s % 2, :]), sc, bc(smax[:, s % 2, :], 2, KEYS),
                                ALU.subtract).then_inc(shifted, 1)

            def take_pv(i, s):
                dve.wait_ge(pv_done, 4 * i + s + 1)
                pv = M[:, 0:UNITS * VP].rearrange("p (u v) -> p u v", v=VP)
                v.reciprocal(rden[:, :], pv[:, :, VP - 1])
                v.tensor_reduce(num[:, :, :], pv[:, :, 0:VP - 1].rearrange("p u (a d) -> p u d a", a=3),
                                axis=AX, op=ALU.add).then_inc(pv_out, 1)
                dve.wait_ge(pv_out, 4 * i + s + 1)
                ca.link(v.tensor_tensor(attn[:, s * UNITS:(s + 1) * UNITS, :], num[:, :, :],
                                        bc(rden[:, :], 2, DH), ALU.mult))

            def weights(f):
                dve.wait_ge(gexp_s, f + 1)
                cf.link(v.tensor_scalar(gden[:, :], gexp[:, :], 1.0, None, ALU.add))
                cf.link(v.reciprocal(gw[:, :, 0], gden[:, :]))
                cf.link(v.tensor_tensor(gw[:, :, 1], gexp[:, :], gw[:, :, 0], ALU.mult))
                for tt in range(TILES):
                    for j in range(2):
                        last = v.tensor_scalar(wsel[:, tt, j, :], iota[:, :], gidf[:, tt, j:j + 1],
                                               gw[:, tt, j:j + 1], ALU.is_equal, ALU.mult)
                cf.link(last)
                if f > 0:
                    dve.wait_ge(coef_s, 4 * f)
                if f > 0:
                    dve.wait_ge(wT_done, f)
                v.tensor_tensor(wexp[:, :, :], wsel[:, :, 0, :], wsel[:, :, 1, :], ALU.add).then_inc(wexp_s, 1)

            def weights_T(f):
                dve.wait_ge(wT_done, f + 1)
                if f > 0:
                    dve.wait_ge(lnb_done, f)
                v.tensor_copy(wexpT[:, :], M[0:EXPERTS, 0:STEP]).then_inc(wT_out, 1)

            def add_ln_b(f):
                dve.wait_ge(lnb_done, f + 1)
                xs = X[:, TILES * f:TILES * (f + 1), :]
                v.tensor_tensor(xs, xs, M[:, 0:STEP].rearrange("p (a d) -> p a d", d=D), ALU.add).then_inc(lnb_out, 1)

            def zsum(f, q):
                dve.wait_ge(sq_s, 4 * f + q + 1)
                if 4 * f + q - 1 > 0:
                    dve.wait_ge(coef_s, 4 * f + q - 1)
                v.reduce_sum(zss[:, q % 2, :], zsq[:, q % 2, :].rearrange("p (e d) -> p e d", d=D),
                             axis=AX).then_inc(ss_s, 1)

            def scale(f, q):
                half, tt, b = q // 2, q % 2, f // PER_BATCH
                dve.wait_ge(coef_s, 4 * f + q + 1)
                if q == 0:
                    if f > 0:
                        dve.wait_ge(y_s, f)
                    if f == 0:
                        dve.wait_ge(lng_s, 2)
                for e in range(HALF):
                    ee = half * HALF + e
                    last = v.scalar_tensor_tensor(ypart[:, tt, ee, :], zB[q % 2][:, e * D:(e + 1) * D],
                                                  zcoef[:, q % 2, e:e + 1], ln_gG[:, b, ee, :], ALU.mult, ALU.mult)
                last.then_inc(u_done, 1)

            def top_two(i):
                dve.wait_ge(gate_done, i + 1)
                v.tensor_copy(gsc[:, :, :], M[:, 0:TILES * EXPERTS].rearrange("p (a e) -> p a e", e=EXPERTS)
                              ).then_inc(g_out, 1)
                dve.wait_ge(g_out, i + 1)
                for tt in range(TILES):
                    last = v.max(gtop[:, tt, :], gsc[:, tt, :])
                ca.link(last)
                for tt in range(TILES):
                    last = v.max_index(gidx[:, tt, :], gtop[:, tt, :], gsc[:, tt, :])
                ca.link(last)
                v.tensor_copy(gidf[:, :, :], gidx[:, :, 0:2])
                if i > 0:
                    dve.wait_ge(gexp_s, i)
                v.tensor_tensor(gdif[:, :], gtop[:, :, 1], gtop[:, :, 0], ALU.subtract).then_inc(gdif_s, 1)

            dve.wait_ge(loaded_w, ALL_W)
            stats_front(0)
            dve.wait_ge(set_act, 1)
            pre.link(v.tensor_scalar(silu_den[:, :], silu_den[:, :], 1.0, None, ALU.add))
            pre.link(v.reciprocal(silu_den[:, :], silu_den[:, :]))
            v.tensor_tensor(silu[:, :], cT[:, :], silu_den[:, :], ALU.mult).then_inc(silu_s, 1)
            normed_front(0)
            pre.link(split(w_qk_hi[:, :, :, :], w_qk_lo[:, :, :, :], w_qk[:, :, :, :]))
            dve.wait_ge(set_pe, 2)
            mod_ps = M[:, 0:4 * BATCH].rearrange("p (j b) -> p j b", b=BATCH)
            v.tensor_scalar(modT[:, 0:4:2, :], mod_ps[:, 0:4:2, :], 0.0, None, ALU.add)
            pre.link(v.tensor_scalar(modT[:, 1:4:2, :], mod_ps[:, 1:4:2, :], 1.0, None, ALU.add))
            v.tensor_copy(ident16[:, :], ident[:, :])
            v.tensor_copy(rep16[:, :], rep[:, :])
            v.tensor_copy(mask16[:, :, :, :], maskf[:, :, :, :]).then_inc(set_att, 1)

            def set_gates():
                gate_ps = zB[0][:, :].rearrange("p (b k d) -> p b k d", b=BATCH, k=2)
                v.tensor_scalar(gate_sign[:, :, :, :], gate_ps, 0.0, 2.0, ALU.is_ge, ALU.mult)
                pre.link(v.tensor_scalar(gates[:, :, :, :], gate_ps, -1.0, 0.25, ALU.mult, ALU.max))
                pre.link(v.tensor_tensor(gates[:, :, :, :], gate_ps, gates[:, :, :, :], ALU.max))
                flat = "p b k d -> p (b k d)"
                v.scalar_tensor_tensor(gates[:, :, :, :].rearrange(flat), gate_sign[:, :, :, :].rearrange(flat),
                                       -1.0, gates[:, :, :, :].rearrange(flat), ALU.add, ALU.mult).then_inc(gates_s, 1)
                dve.wait_ge(gates_s, 1)
                v.tensor_tensor(w_oG[:, :, :], bc(w_o[:, :], 1, BATCH), gates[:, :, 0, :], ALU.mult)
                pre.link(v.tensor_tensor(b_oG[:, :, :], bc(b_o[:, :], 1, BATCH), gates[0:1, :, 0, :], ALU.mult))

            def set_ffn_bias():
                dve.wait_ge(loaded_f, ALL_F)
                v.tensor_copy(ones_r[:, :], ones[:, :])
                v.tensor_copy(center_r[:, :], center[:, :])
                pre.link(v.reduce_sum(b2_mean[:, :], b2[:, :, :], axis=AX))
                pre.link(v.tensor_scalar(b2_mean[:, :], b2_mean[:, :], 1.0 / D, None, ALU.mult))
                pre.link(v.tensor_tensor(b2[:, :, :], b2[:, :, :], bc(b2_mean[:, :], 2, D), ALU.subtract))
                split(b2_rows[0:1, :, :], b2_low[:, :, :], b2[:, :, :]).then_inc(set_b2, 1)

            def set_w2():
                pre.link(v.reduce_sum(w2_mean[:, :], w2[:, :, :], axis=AX))
                pre.link(v.tensor_scalar(w2_mean[:, :], w2_mean[:, :], 1.0 / D, None, ALU.mult))
                v.tensor_tensor(w2[:, :, :], w2[:, :, :], bc(w2_mean[:, :], 2, D), ALU.subtract).then_inc(w2_s, 1)

            def front(n):
                take_hT(n)
                for g in range(GROUPS):
                    low_k(n, g)
                rest_v(n, 0)
                for j in range(2):
                    low_q(n, j)
                    mask_q(n, j)
                rest_v(n, 1)
                set_gates()

            def body(i, att, ffn, nxt):
                n, f = i + 1, i - 1
                if att:
                    shift(i, 0)
                    shift(i, 1)
                if i == 0:
                    set_ffn_bias()
                if ffn:
                    weights(f)
                if nxt:
                    stats_front(n)
                if ffn:
                    zsum(f, 0)
                    weights_T(f)
                if nxt:
                    normed_front(n)
                if att:
                    shift(i, 2)
                if ffn:
                    scale(f, 0)
                    add_ln_b(f)
                    zsum(f, 1)
                if nxt:
                    take_hT(n)
                if att:
                    take_pv(i, 0)
                    shift(i, 3)
                if i == 0:
                    set_w2()
                if ffn:
                    scale(f, 1)
                    zsum(f, 2)
                if nxt:
                    low_k(n, 0)
                    low_k(n, 1)
                if ffn:
                    scale(f, 2)
                if att:
                    take_pv(i, 1)
                if nxt:
                    low_k(n, 2)
                    low_k(n, 3)
                if att:
                    take_pv(i, 2)
                    take_pv(i, 3)
                    ca.link(v.transpose(attnT[:, :], attn[:, :, :].rearrange("p n d -> p (n d)")))
                    if i > 0:
                        dve.wait_ge(o_done, i)
                    v.tensor_scalar(attnTb[:, :], attnT[:, :], b_v[:, :], None, ALU.add).then_inc(attn_ready, 1)
                if nxt:
                    rest_v(n, 0)
                    low_q(n, 0)
                if att:
                    b = i // PER_BATCH
                    dve.wait_ge(o_done, i + 1)
                    xs = X[:, TILES * i:TILES * (i + 1), :]
                    v.tensor_tensor(xs, xs, M[:, 0:STEP].rearrange("p (a d) -> p a d", d=D), ALU.add).then_inc(x1_s, 1)
                    dve.wait_ge(x1_s, i + 1)
                    norm_stats(ca, TILES * i, mv2).then_inc(stats2, 1)
                if nxt:
                    mask_q(n, 0)
                if att:
                    dve.wait_ge(rstd2_s, i + 1)
                    if i > 0:
                        dve.wait_ge(x2T_s, i)
                    normed(xn2, TILES * i, mv2, rstd2).then_inc(xn2_s, 1)
                if ffn:
                    zsum(f, 3)
                if att:
                    dve.wait_ge(x2T_s, i + 1)
                    ca.link(v.tensor_scalar(h2T[:, :], M[:, 0:STEP], modT[:, 3, b:b + 1],
                                            modT[:, 2, b:b + 1], ALU.mult, ALU.add))
                    ca.link(v.tensor_copy(h2_hi[:, :], h2T[:, :]))
                    v.tensor_tensor(h2_lo[:, :], h2T[:, :], h2_hi[:, :].bitcast(fp32), ALU.subtract).then_inc(h2_s, 1)
                if nxt:
                    low_q(n, 1)
                    rest_v(n, 1)
                if ffn:
                    scale(f, 3)
                if nxt:
                    mask_q(n, 1)
                if att:
                    top_two(i)

            steps(front, body)

        @block.tensor
        def _(pe):
            mm, tr = nc.tensor.matmul, nc.tensor.transpose

            def three(outp, a_hi, a_lo, b_hi, b_lo):
                mm(outp, a_hi, b_hi, start=True, stop=False)
                mm(outp, a_hi, b_lo, start=False, stop=False)
                return mm(outp, a_lo, b_hi, start=False, stop=True)

            pe.wait_ge(silu_s, 1)
            for n, j in enumerate((0, 1, 3, 4)):
                last = mm(M[:, n * BATCH:(n + 1) * BATCH], w_mod[:, j, :], silu[:, :], start=True, stop=True)
            last.then_inc(set_pe, 1)
            for b in range(BATCH):
                for n, j in enumerate((2, 5)):
                    at = (2 * b + n) * D
                    last = mm(zB[0][:, at:at + D], silu[:, b:b + 1].to_broadcast([P, P]), w_mod[:, j, :],
                              start=True, stop=True)
            last.then_inc(set_pe, 1)

            def turn_x(n):
                pe.wait_ge(xn1_s, n + 1)
                if 8 * n - 8 > 0:
                    pe.wait_ge(gelu_s, 8 * n - 8)
                for tt in range(TILES):
                    last = tr(U[0][:, tt * P:(tt + 1) * P], xn1[:, tt, :], ident[:, :])
                last.then_inc(xT_s, 1)

            def proj_k(n, g):
                if g == 0:
                    pe.wait_ge(hT_s, n + 1)
                if g > 1:
                    if 4 * n + g - 1 > 0:
                        pe.wait_ge(k_ready, 4 * n + g - 1)
                three(U[(g + 1) % 2][0:3 * GC, 0:SPAN], w_qk_hi[:, 1, g, :], w_qk_lo[:, 1, g, :], hT_hi[:, :],
                      hT_lo[:, :]).then_inc(kq_proj, 1)

            def proj_q(n, j):
                if j == 0:
                    pe.wait_ge(k_ready, 4 * n + 4)
                else:
                    pe.wait_ge(v_out, 2 * n + 1)
                for g in (2 * j, 2 * j + 1):
                    last = three(U[j][0:3 * GC, (g % 2) * STEP:(g % 2 + 1) * STEP], w_qk_hi[:, 0, g, :],
                                 w_qk_lo[:, 0, g, :], hT_hi[:, BLK:SPAN], hT_lo[:, BLK:SPAN])
                last.then_inc(kq_proj, 1)

            def proj_v(n, j):
                if j == 0:
                    pe.wait_ge(k_ready, 4 * n + 3)
                else:
                    pe.wait_ge(q_lo_s, 2 * n + 1)
                for m in range(4):
                    at = BLK * (4 * j + m)
                    for r in range(2):
                        last = mm(U[1 - j][r * KEYS:(r + 1) * KEYS, m * D:(m + 1) * D], hT[:, at:at + KEYS],
                                  w_v[:, :], start=True, stop=True)
                last.then_inc(v_proj, 1)

            def up(i, e, nxt):
                if e == 0:
                    pe.wait_ge(h2_s, i + 1)
                if e < 2 and nxt:
                    if e == 0:
                        pe.wait_ge(q_lo_s, 2 * i + 4)
                    else:
                        pe.wait_ge(v_out, 2 * i + 4)
                elif e < 2:
                    if i > 0:
                        pe.wait_ge(gelu_s, 8 * i)
                else:
                    if 8 * i + e - 1 > 0:
                        pe.wait_ge(gelu_s, 8 * i + e - 1)
                for c in range(CH):
                    last = three(U[(e + 1) % 2][:, c * STEP:(c + 1) * STEP], w1_hi[:, e, c, :], w1_lo[:, e, c, :],
                                 h2_hi[:, :], h2_lo[:, :])
                last.then_inc(up_done, 1)

            def scores(i, s):
                if s == 0:
                    pe.wait_ge(k_ready, 4 * i + 4)
                    pe.wait_ge(q_vec, 2 * i + 2)
                    pe.wait_ge(q_pool, 2 * i + 2)
                if 4 * i + s - 1 > 0:
                    pe.wait_ge(shifted, 4 * i + s - 1)
                which = mask16[:, i if s == 0 else STEPS, :, :]
                bank = scoreB[s % 2]
                mm(bank[:, :].rearrange("p (b g k) -> p b g k", b=2, g=GROUPS), rep16[:, :],
                   bc(which, 2, GROUPS), start=True, stop=False, skip_group_check=True)
                for u in range(UNITS):
                    blk, g = 2 * s + u // GROUPS, u % GROUPS
                    last = mm(bank[:, u * KEYS:(u + 1) * KEYS], q_st[:, g, blk, :, :].rearrange("p h q -> p (h q)"),
                              k_st[:, g, blk * BLK:blk * BLK + KEYS], start=False, stop=u == UNITS - 1,
                              skip_group_check=True)
                last.then_inc(scored, 1)

            def turn(i, s):
                pe.wait_ge(p_ready, 4 * i + s + 1)
                if 4 * i + s > 0:
                    pe.wait_ge(p_out, 4 * i + s)
                for u in range(UNITS):
                    last = tr(probTB[:, u * P:(u + 1) * P],
                              prob_hl[:, s % 2, u, :, :].rearrange("p a k -> p (a k)"), ident16[:, :])
                last.then_inc(p_turned, 1)

            def values(i, s):
                pe.wait_ge(p_out, 4 * i + s + 1)
                pe.wait_ge(v_ready, 2 * i + 1 + s // 2)
                if s > 0:
                    if 4 * i + s > 0:
                        pe.wait_ge(pv_out, 4 * i + s)
                elif i > 0:
                    if i > 0:
                        pe.wait_ge(lnb_out, i)
                for u in range(UNITS):
                    blk, g = 2 * s + u // GROUPS, u % GROUPS
                    for h in range(HG):
                        last = mm(M[h * BLK:(h + 1) * BLK, u * VP:(u + 1) * VP],
                                  probT[:, s % 2, u * P + h * BLK:u * P + (h + 1) * BLK],
                                  v_parts[:, blk, HG * g + h, :], start=True, stop=True)
                last.then_inc(pv_done, 1)

            def down(f, q):
                half, tt = q // 2, q % 2
                pe.wait_ge(gelu_s, 8 * f + HALF * (half + 1))
                if 4 * f + q - 1 > 0:
                    pe.wait_ge(u_done, 4 * f + q - 1)
                bank, tok = zB[q % 2], slice(tt * P, (tt + 1) * P)
                by_e = bank[:, :].rearrange("p (e d) -> p e d", d=D)
                mm(by_e, h2_hi[:, tok], bc(center_r[:, :], 1, HALF), start=True, stop=False, skip_group_check=True)
                mm(by_e, h2_lo[:, tok], bc(center_r[:, :], 1, HALF), start=False, stop=False, skip_group_check=True)
                mm(by_e, ones_r[:, :], b2_rows[:, half * HALF:(half + 1) * HALF, :], start=False, stop=False,
                   skip_group_check=True)
                for e in range(HALF):
                    ee = half * HALF + e
                    for c in range(CH):
                        last = mm(bank[:, e * D:(e + 1) * D], hid[:, ee, c, tok], w2[:, ee * CH + c, :],
                                  start=False, stop=e == HALF - 1 and c == CH - 1, skip_group_check=True)
                last.then_inc(z_done, 1)

            def turn_weights(f):
                pe.wait_ge(wexp_s, f + 1)
                for tt in range(TILES):
                    last = tr(M[0:EXPERTS, tt * P:(tt + 1) * P], wexp[:, tt, :], ident[:, :])
                last.then_inc(wT_done, 1)

            def ln_b_sum(f):
                pe.wait_ge(wT_out, f + 1)
                for tt in range(TILES):
                    last = mm(M[:, tt * D:(tt + 1) * D], wexpT[:, tt * P:(tt + 1) * P], ln_bG[:, f // PER_BATCH, :],
                              start=True, stop=True)
                last.then_inc(lnb_done, 1)

            def front(n):
                turn_x(n)
                for g in range(GROUPS):
                    proj_k(n, g)
                proj_v(n, 0)
                proj_q(n, 0)
                proj_q(n, 1)
                proj_v(n, 1)

            def body(i, att, ffn, nxt):
                n, f = i + 1, i - 1
                if att:
                    scores(i, 0)
                    scores(i, 1)
                if i == 1:
                    pe.wait_ge(w2_s, 1)
                    pe.wait_ge(b2_low_moved, 16)
                    pe.wait_ge(lng_s, 2)
                if ffn:
                    down(f, 0)
                    turn_weights(f)
                if att:
                    turn(i, 0)
                    scores(i, 2)
                if ffn:
                    ln_b_sum(f)
                    down(f, 1)
                if nxt:
                    turn_x(n)
                if att:
                    turn(i, 1)
                    values(i, 0)
                    scores(i, 3)
                if ffn:
                    down(f, 2)
                if nxt:
                    proj_k(n, 0)
                    proj_k(n, 1)
                if att:
                    turn(i, 2)
                    values(i, 1)
                if nxt:
                    proj_k(n, 2)
                    proj_k(n, 3)
                if att:
                    turn(i, 3)
                    values(i, 2)
                    values(i, 3)
                if nxt:
                    proj_v(n, 0)
                    proj_q(n, 0)
                if att:
                    b = i // PER_BATCH
                    if i == 0:
                        pe.wait_ge(w1_lo_s, 2)
                        pe.wait_ge(set_pool, 1)
                    pe.wait_ge(attn_ready, i + 1)
                    for tt in range(TILES):
                        o = M[:, tt * D:(tt + 1) * D]
                        mm(o, attnTb[:, tt * P:(tt + 1) * P], w_oG[:, b, :], start=True, stop=False)
                        last = mm(o, ones[0:1, :], b_oG[:, b, :], start=False, stop=True)
                    last.then_inc(o_done, 1)
                if ffn:
                    down(f, 3)
                if att:
                    pe.wait_ge(xn2_s, i + 1)
                    for tt in range(TILES):
                        last = tr(M[:, tt * P:(tt + 1) * P], xn2[:, tt, :], ident[:, :])
                    last.then_inc(x2T_s, 1)
                if nxt:
                    proj_q(n, 1)
                    proj_v(n, 1)
                if att:
                    up(i, 0, nxt)
                    for tt in range(TILES):
                        last = mm(M[:, tt * EXPERTS:(tt + 1) * EXPERTS], h2T[:, tt * P:(tt + 1) * P], w_gate[:, :],
                                  start=True, stop=True)
                    last.then_inc(gate_done, 1)
                    for e in range(1, EXPERTS):
                        up(i, e, nxt)

            steps(front, body)


def kernel(**inputs):
    import concourse.bacc as bacc
    from concourse.bass_utils import run_bass_kernel_spmd

    def a(name):
        return np.asarray(inputs["L0_" + name])

    def by_group(w):
        w = w.reshape(w.shape[0], GROUPS, 1, GC)
        return np.broadcast_to(w, (w.shape[0], GROUPS, 3, GC)).reshape(w.shape[0], GROUPS, 3 * GC)

    order = np.arange(D).reshape(GROUPS, HG, DH).transpose(1, 0, 2).reshape(D)
    w_qk = np.stack([by_group(a("attn_q_w").T), by_group(a("attn_k_w").T)], 1)
    b_qk = np.stack([by_group(a("attn_q_b")[None]), by_group(a("attn_k_b")[None])], 1)[0].transpose(2, 0, 1)
    j, k = np.arange(BLK)[:, None], np.arange(KEYS)[None, :]
    inner = np.where((k > j) & (k <= j + BLK), 0.0, -1e30)
    first = np.where((k > j) & (k <= j + BLK) & (k >= BLK), 0.0, -1e30)
    masks = np.stack([np.stack([first if s % PER_BATCH == 0 and s < STEPS else inner, inner], 1)
                      for s in range(STEPS + 1)], 1)
    f4 = np.float32
    arrays = {
        "x": a("attn_x"), "w_qk": w_qk, "b_qk": b_qk, "w_v": a("attn_v_w").T,
        "b_v": a("attn_v_b")[order][:, None], "w_o": a("attn_o_w").T[order], "b_o": a("attn_o_b")[None],
        "w_mod": a("wmod").reshape(D, 6, D), "cT": a("c").T,
        "ident": np.eye(P, dtype=f4), "rep": np.tile(np.eye(BLK, dtype=f4), (1, HG)), "masks": masks.astype(f4),
        "headmask": (np.arange(3 * GC)[:, None] % GC // DH == np.arange(HG)[None, :]).astype(f4),
        "iota": np.broadcast_to(np.arange(EXPERTS, dtype=f4), (P, EXPERTS)),
        "center": (np.eye(D) - 1.0 / D).astype(f4),
        "w_gate": a("ffn_gate_w"), "w1": a("ffn_w1").reshape(EXPERTS, D, CH, P).transpose(1, 0, 2, 3),
        "b1": a("ffn_b1").reshape(EXPERTS, CH, P).transpose(2, 0, 1),
        "w2": a("ffn_w2").reshape(EXPERTS * CH, P, D).transpose(1, 0, 2), "b2": a("ffn_b2")[None],
        "ln_g": a("ffn_ln_g"), "ln_b": a("ffn_ln_b"),
    }
    arrays = {name: np.ascontiguousarray(x) for name, x in arrays.items()}
    nc = bacc.Bacc("TRN2", target_bir_lowering=False, num_devices=1)
    dram = {name: nc.dram_tensor(f"in_{name}", x.shape, mybir.dt.from_np(x.dtype), kind="ExternalInput").ap()
            for name, x in arrays.items()}
    out = nc.dram_tensor("out_x", (BATCH, SEQ, D), mybir.dt.float32, kind="ExternalOutput").ap()
    build(nc, dram, out)
    r = run_bass_kernel_spmd(nc, [{f"in_{name}": x for name, x in arrays.items()}], core_ids=[0])
    return r.results[0]["out_x"]
```

```python
import numpy as np
import concourse.bass as bass
from concourse import mybir
from contextlib import ExitStack

BATCH, SEQ, D = 2, 1024, 128
HEADS, DH, WINDOW = 16, 8, 32
EXPERTS, FF = 8, 256
P = 128
STEP = 256
TILES = STEP // P
STEPS = BATCH * SEQ // STEP
PER_BATCH = SEQ // STEP
BLK = WINDOW
KEYS = 2 * BLK
NBLK = STEP // BLK
GROUPS, HG = 4, 4
GC = HG * DH
SPAN = BLK + STEP
QUARTERS = 4
UNITS = 2 * GROUPS
CH = FF // P
HALF = EXPERTS // 2
VP = 3 * DH + 1
LN1_EPS, LN2_EPS, FFN_EPS = 1e-5, 1e-5, 1e-6


def build(nc, t, out):
    fp32, f32r = mybir.dt.float32, mybir.dt.float32r
    bf16, fp16, u32 = mybir.dt.bfloat16, mybir.dt.float16, mybir.dt.uint32
    ALU = mybir.AluOpType
    ACT = mybir.ActivationFunctionType
    AX = mybir.AxisListType.X

    ctx = ExitStack()
    with ctx:
        def sb(name, shape, dt=fp32):
            return ctx.enter_context(nc.sbuf_tensor(name, shape, dt))

        def sem(name):
            return ctx.enter_context(nc.semaphore(name))

        X = sb("x_tokens", [P, STEPS * TILES, D])
        PACKS = {"mod": ((("cT", (BATCH,)), ("w_mod", (6, D))), P),
                 "proj": ((("ident", (P,)), ("b_qk", (2, GROUPS)), ("w_qk", (2, GROUPS, 3 * GC))), P),
                 "att": ((("w_v", (D,)), ("headmask", (HG,)), ("b_v", (1,)), ("w_o", (D,))), P),
                 "mask": ((("rep", (P,)), ("masks", (STEPS + 1, 2, KEYS))), BLK),
                 "ffn": ((("center", (D,)), ("iota", (EXPERTS,)), ("w_gate", (EXPERTS,)), ("b1", (EXPERTS, CH))), P)}
        packs, part = {}, {}
        for name, (parts, rows) in PACKS.items():
            packs[name] = sb("pack_" + name, [rows, sum(int(np.prod(shape)) for _, shape in parts)])
            at = 0
            for item, shape in parts:
                size = int(np.prod(shape))
                view = packs[name][:, at:at + size]
                if len(shape) == 2:
                    view = view.rearrange("p (a b) -> p a b", b=shape[1])
                if len(shape) == 3:
                    view = view.rearrange("p (a b c) -> p a b c", b=shape[1], c=shape[2])
                part[item] = view
                at += size
        cT, w_mod, ident, b_qk, w_qk = part["cT"], part["w_mod"], part["ident"], part["b_qk"][0:3 * GC, :, :], part["w_qk"]
        w_v, headmask, b_v, w_o = part["w_v"], part["headmask"][0:3 * GC, :], part["b_v"], part["w_o"]
        rep, maskf = part["rep"], part["masks"]
        center, iota, w_gate, b1 = part["center"], part["iota"], part["w_gate"], part["b1"]
        w_qk_hi = sb("w_qk_hi", [P, 2, GROUPS, 3 * GC], f32r)
        w_qk_lo = sb("w_qk_lo", [P, 2, GROUPS, 3 * GC], f32r)
        b_o = sb("b_o", [P, D])
        w1 = sb("w1", [P, EXPERTS, CH, P])
        w1_hi = sb("w1_hi", [P, EXPERTS, CH, P], f32r)
        w1_lo = sb("w1_lo", [P, EXPERTS, CH, P], f32r)
        w2 = sb("w2", [P, EXPERTS * CH, D])
        w2_mean = sb("w2_mean", [P, EXPERTS * CH])
        b2 = sb("b2", [EXPERTS, D])
        b2_mean = sb("b2_mean", [EXPERTS, 1])
        b2_rows = sb("b2_rows", [2, EXPERTS, D], f32r)
        b2_high = sb("b2_high", [EXPERTS, D], f32r)
        b2_low = sb("b2_low", [EXPERTS, D], f32r)
        ln_g = sb("ln_g", [P, EXPERTS, D])
        ln_b = sb("ln_b", [EXPERTS, D])
        ident16 = sb("ident16", [P, P], fp16)
        center_r = sb("center_r", [P, D], f32r)
        rep16 = sb("rep16", [BLK, P], bf16)
        mask16 = sb("mask16", [BLK, STEPS + 1, 2, KEYS], bf16)
        ones = sb("ones", [2, P])
        one = sb("one", [P, 1])
        idle = sb("idle", [P, 512], bf16)
        table = sb("table", [P, 1])
        ones_r = sb("ones_r", [2, P], f32r)
        mhalf = sb("mhalf", [P, 8])
        silu = sb("silu", [P, BATCH])
        silu_den = sb("silu_den", [P, BATCH])
        modT = sb("modT", [P, 4, BATCH])
        gates = sb("gates", [P, BATCH, 2, D])
        gate_sign = sb("gate_sign", [P, BATCH, 2, D])
        w_oG = sb("w_oG", [P, BATCH, D])
        b_oG = sb("b_oG", [P, BATCH, D])
        ln_gG = sb("ln_gG", [P, BATCH, EXPERTS, D])
        ln_bG = sb("ln_bG", [EXPERTS, BATCH, D])
        stats = sb("stats", [P, TILES, 6])
        mv1 = sb("mv1", [P, TILES, 2])
        mv2 = sb("mv2", [P, TILES, 2])
        var1 = sb("var1", [P, TILES])
        var2 = sb("var2", [P, TILES])
        rstd1 = sb("rstd1", [P, TILES])
        rstd2 = sb("rstd2", [P, TILES])
        xn1 = sb("xn1", [P, TILES, D])
        xn2 = sb("xn2", [P, TILES, D])
        hT = sb("hT", [P, SPAN])
        hT2 = sb("hT2", [P, NBLK, 2, KEYS])
        hT_hi = sb("hT_hi", [P, SPAN], f32r)
        hT_lo = sb("hT_lo", [P, SPAN], f32r)
        k_st = sb("k_st", [3 * GC, GROUPS, SPAN], f32r)
        q_hl = sb("q_hl", [3 * GC, GROUPS, STEP], f32r)
        q_st = sb("q_st", [3 * GC, GROUPS, NBLK, HG, BLK], f32r)
        v_rest = sb("v_rest", [P, 2, 4 * D])
        v_parts = sb("v_parts", [P, NBLK, HEADS, VP], bf16)
        smax = sb("smax", [P, 2, UNITS])
        sdif = sb("sdif", [P, QUARTERS, UNITS * KEYS])
        prob = sb("prob", [P, QUARTERS, UNITS * KEYS])
        prob_hl = sb("prob_hl", [P, QUARTERS, UNITS, 2, KEYS], fp16)
        probT = sb("probT", [P, 2, UNITS * P], fp16)
        rden = sb("rden", [P, UNITS])
        num = sb("num", [P, UNITS, DH])
        attn = sb("attn", [P, NBLK * GROUPS, DH])
        attnT = sb("attnT", [P, STEP])
        attnTb = sb("attnTb", [P, STEP])
        h2T = sb("h2T", [P, STEP])
        h2_hi = sb("h2_hi", [P, 2, STEP], f32r)
        h2_lo = sb("h2_lo", [P, 2, STEP], f32r)
        gsc = sb("gsc", [P, TILES, EXPERTS])
        gtop = sb("gtop", [P, TILES, 8])
        gidx = sb("gidx", [P, TILES, 8], u32)
        gidf = sb("gidf", [P, TILES, 2])
        gdif = sb("gdif", [P, TILES])
        gexp = sb("gexp", [P, TILES])
        gden = sb("gden", [P, TILES])
        gw = sb("gw", [P, TILES, 2])
        wsel = sb("wsel", [P, TILES, 2, EXPERTS])
        wexp = sb("wexp", [P, TILES, EXPERTS])
        wexpT = sb("wexpT", [EXPERTS, STEP])
        hid = sb("hid", [P, EXPERTS, CH, STEP])
        zsq = sb("zsq", [P, 2, HALF * D])
        zss = sb("zss", [P, 2, HALF])
        zvar = sb("zvar", [P, 2, HALF])
        zrstd = sb("zrstd", [P, 2, HALF])
        zcoef = sb("zcoef", [P, 2, HALF])
        ypart = sb("ypart", [P, TILES, EXPERTS, D])
        yout = sb("yout", [P, TILES, D])

        def bank(name, shape=(P, 512), dt=fp32):
            return ctx.enter_context(nc.psum_tensor(name, list(shape), dt))

        scoreB = [bank("score0"), bank("score1")]
        probTB = bank("probT_bank", (P, 1024), fp16)
        U = [bank("turns0"), bank("turns1")]
        zB = [bank("z0"), bank("z1")]
        M = bank("misc")

        loaded_x, loaded_mod, loaded_proj = sem("loaded_x"), sem("loaded_mod"), sem("loaded_proj")
        loaded_att, loaded_mask, loaded_bo = sem("loaded_att"), sem("loaded_mask"), sem("loaded_bo")
        loaded_ffn, loaded_f, loaded_rest = sem("loaded_ffn"), sem("loaded_f"), sem("loaded_rest")
        b2_moved = sem("b2_moved")
        set_pool, set_act, set_pe = sem("set_pool"), sem("set_act"), sem("set_pe")
        set_vec, set_b2, set_att, silu_s = sem("set_vec"), sem("set_b2"), sem("set_att"), sem("silu_s")
        w1_hi_s, w1_lo_s, w2_s, lng_s, gates_s = sem("w1_hi_s"), sem("w1_lo_s"), sem("w2_s"), sem("lng_s"), sem("gates_s")
        v_front, v_att, v_ffn = sem("v_front"), sem("v_att"), sem("v_ffn")
        p_front, p_att, p_ffn = sem("p_front"), sem("p_att"), sem("p_ffn")
        stats1, rstd1_s, xn1_s, xT_s = sem("stats1"), sem("rstd1_s"), sem("xn1_s"), sem("xT_s")
        hT_hi_s, hT_s = sem("hT_hi_s"), sem("hT_s")
        kq_proj, kq_hi, k_ready = sem("kq_proj"), sem("kq_hi"), sem("k_ready")
        q_lo_s, q_vec, q_pool = sem("q_lo_s"), sem("q_vec"), sem("q_pool")
        v_proj, v_hi_s, v_out, v_ready = sem("v_proj"), sem("v_hi_s"), sem("v_out"), sem("v_ready")
        scored, shifted, exped, p_ready = sem("scored"), sem("shifted"), sem("exped"), sem("p_ready")
        p_turned, p_out, pv_done, pv_out = sem("p_turned"), sem("p_out"), sem("pv_done"), sem("pv_out")
        attn_ready, o_done, x1_s = sem("attn_ready"), sem("o_done"), sem("x1_s")
        stats2, rstd2_s, xn2_s, x2T_s = sem("stats2"), sem("rstd2_s"), sem("xn2_s"), sem("x2T_s")
        h2_s = sem("h2_s")
        gate_done, g_out, gdif_s, gexp_s, wexp_s = sem("gate_done"), sem("g_out"), sem("gdif_s"), sem("gexp_s"), sem("wexp_s")
        wT_done, wT_out, lnb_done, lnb_out = sem("wT_done"), sem("wT_out"), sem("lnb_done"), sem("lnb_out")
        up_done, gelu_s, z_done, sq_s = sem("up_done"), sem("gelu_s"), sem("z_done"), sem("sq_s")
        ss_s, coef_s, u_done, y_s = sem("ss_s"), sem("coef_s"), sem("u_done"), sem("y_s")
        stored, b_o_s, xb_s, hT2_s = sem("stored"), sem("b_o_s"), sem("xb_s"), sem("hT2_s")
        ss_act = sem("ss_act")
        y_last = sem("y_last")
        w2_mean_s = sem("w2_mean_s")
        mask_s, set_idle = sem("mask_s"), sem("set_idle")

        block = ctx.enter_context(nc.Block())

        def bc(ap, dim, n):
            return ap.unsqueeze(dim).to_broadcast([*ap.shape[:dim], n, *ap.shape[dim:]])

        def z_bank(f, q):
            return scoreB[q % 2] if f == STEPS - 1 and q > 1 else zB[q % 2]

        def blocks(ap):
            return ap.rearrange("p g (b q) -> p g b q", q=BLK)

        def by_key(ap):
            return ap.rearrange("p (u k) -> p u k", k=KEYS)

        def steps(front, body):
            front(0)
            for i in range(STEPS + 1):
                body(i, i < STEPS, i > 0, i + 1 < STEPS)

        class Chain:

            def __init__(self, eng, s):
                self.eng, self.s, self.n = eng, s, 0

            def link(self, ins):
                self.n += 1
                ins.then_inc(self.s, 1)
                self.eng.wait_ge(self.s, self.n)

        F_LOADS = [(w1, "w1"), (w2, "w2"), (b2, "b2"), (ln_b, "ln_b")]
        ALL_F = 16 * (len(F_LOADS) + 1)
        x_view = t["x"].rearrange("b (n p) d -> p (b n) d", p=P)
        out_view = out.rearrange("b (n p) d -> p (b n) d", p=P)

        def whole(a):
            return a[tuple(slice(None) for _ in a.shape)]

        @block.sync
        def _(sp):
            def load_pack(name, signal):
                sp.dma_start(packs[name][:, :], t["pack_" + name]).then_inc(signal, 16)

            load_pack("mod", loaded_mod)
            sp.dma_start(X[:, 0:TILES, :], x_view[:, 0:TILES, :]).then_inc(loaded_x, 16)
            load_pack("proj", loaded_proj)
            load_pack("att", loaded_att)
            load_pack("mask", loaded_mask)
            sp.dma_start(X[:, TILES:, :], x_view[:, TILES:, :]).then_inc(loaded_rest, 16)
            sp.dma_start(b_o[:, :], t["b_o"].partition_broadcast(P)).then_inc(loaded_bo, 16)
            load_pack("ffn", loaded_ffn)
            for dst, name in F_LOADS:
                sp.dma_start(whole(dst), t[name]).then_inc(loaded_f, 16)
            sp.dma_start(ln_g[:, :, :], t["ln_g"].rearrange("e d -> (e d)").partition_broadcast(P)
                         .rearrange("p (e d) -> p e d", e=EXPERTS)).then_inc(loaded_f, 16)
            sp.wait_ge(set_b2, 1)
            for row, part_of_b2 in enumerate((b2_high, b2_low)):
                sp.dma_start(b2_rows[row:row + 1, :, :].bitcast(fp32), part_of_b2[:, :].bitcast(fp32)
                             ).then_inc(b2_moved, 16)
            for f in range(STEPS):
                sp.wait_ge(y_s, f + 1)
                if f == STEPS - 1:
                    sp.wait_ge(y_last, 1)
                sp.dma_start(out_view[:, TILES * f:TILES * (f + 1), :], yout[:, :, :]).then_inc(stored, 16)
            sp.wait_ge(stored, 16 * STEPS)

        @block.gpsimd
        def _(pool):
            g = nc.gpsimd
            cn, ca, cf = Chain(pool, p_front), Chain(pool, p_att), Chain(pool, p_ffn)
            g.memset(mhalf[:, :], -0.5)
            g.memset(one[:, :], 1.0)
            g.memset(ones[:, :], 1.0)
            g.memset(v_parts[:, :, :, VP - 1:VP], 1.0)
            g.memset(hT[:, STEP:SPAN], 0.0).then_inc(set_pool, 1)
            pool.wait_ge(set_pool, 1)

            def rstd_front(n):
                pool.wait_ge(stats1, n + 1)
                cn.link(g.tensor_scalar(var1[:, :], mv1[:, :, 1], LN1_EPS, None, ALU.add))
                g.tensor_tensor(rstd1[:, :], var1[:, :], mhalf[:, 0:TILES], ALU.pow).then_inc(rstd1_s, 1)

            def add_b_o(n):
                pool.wait_ge(xn1_s, n + 1)
                if n == 0:
                    pool.wait_ge(b_o_s, 1)
                xs = X[:, TILES * n:TILES * (n + 1), :]
                g.tensor_tensor(xs, xs, bc(b_oG[:, n // PER_BATCH, :], 1, TILES), ALU.add).then_inc(xb_s, 1)

            def split_v(n, j):
                pool.wait_ge(v_out, 2 * n + j + 1)
                vp = v_parts[:, 4 * j:4 * j + 4, :, :].rearrange("p b h v -> p (b h) v")
                vr = v_rest[:, j, :].rearrange("p (n d) -> p n d", d=DH)
                cn.link(g.tensor_tensor(vp[:, :, DH:2 * DH], vr, one[:, :].unsqueeze(2).to_broadcast([P, 4 * HEADS, DH]), ALU.mult))
                g.tensor_tensor(vp[:, :, 2 * DH:3 * DH], vr, vp[:, :, DH:2 * DH], ALU.subtract).then_inc(v_ready, 1)

            def mask_q(n, j):
                pool.wait_ge(q_lo_s, 2 * n + j + 1)
                gg, h = slice(2 * j, 2 * j + 2), HG - 1
                keep = headmask[:, h:h + 1].unsqueeze(2).unsqueeze(3).to_broadcast([3 * GC, 2, NBLK, BLK])
                g.tensor_tensor(q_st[:, gg, :, h, :], blocks(q_hl[:, gg, :].bitcast(fp32)), keep,
                                ALU.mult).then_inc(q_pool, 1)

            def low_prob(i, s):
                pool.wait_ge(exped, 4 * i + s + 1)
                g.tensor_tensor(prob_hl[:, s, :, 1, :], by_key(prob[:, s, :]), prob_hl[:, s, :, 0, :],
                                ALU.subtract).then_inc(p_ready, 1)

            def coefficients(f, q):
                half, tt, b = q // 2, q % 2, q % 2
                if f == STEPS - 1:
                    pool.wait_ge(ss_act, 2 * f + q + 1)
                elif q < 2:
                    pool.wait_ge(ss_s, 2 * f + q + 1)
                else:
                    if 2 * f + q - 1 > 0:
                        pool.wait_ge(ss_act, 2 * f + q - 1)
                cf.link(g.tensor_scalar(zvar[:, b, :], zss[:, b, :], 1.0 / D, FFN_EPS, ALU.mult, ALU.add))
                cf.link(g.tensor_tensor(zrstd[:, b, :], zvar[:, b, :], mhalf[:, 0:HALF], ALU.pow))
                pool.wait_ge(wexp_s, f + 1)
                if 4 * f + q - 1 > 0:
                    pool.wait_ge(u_done, 4 * f + q - 1)
                g.tensor_tensor(zcoef[:, b, :], zrstd[:, b, :], wexp[:, tt, half * HALF:(half + 1) * HALF],
                                ALU.mult).then_inc(coef_s, 1)

            def add_experts(f, q):
                half, tt = q // 2, q % 2
                at = half * HALF
                pool.wait_ge(u_done, 4 * f + q + 1)
                for n in (2, 1):
                    cf.link(g.tensor_tensor(ypart[:, tt, at:at + n, :], ypart[:, tt, at:at + n, :],
                                            ypart[:, tt, at + n:at + 2 * n, :], ALU.add))
                if half == 1:
                    cf.link(g.tensor_tensor(ypart[:, tt, 0, :], ypart[:, tt, 0, :], ypart[:, tt, at, :], ALU.add))
                    pool.wait_ge(lnb_out, f + 1)
                    if tt == 0:
                        if f > 0:
                            pool.wait_ge(stored, 16 * f)
                    last = g.tensor_tensor(yout[:, tt, :], ypart[:, tt, 0, :], X[:, TILES * f + tt, :], ALU.add)
                    if tt == 1:
                        last.then_inc(y_s, 1)
                    elif f == STEPS - 1:
                        last.then_inc(y_last, 1)

            def rstd_second(i):
                pool.wait_ge(stats2, i + 1)
                ca.link(g.tensor_scalar(var2[:, :], mv2[:, :, 1], LN2_EPS, None, ALU.add))
                g.tensor_tensor(rstd2[:, :], var2[:, :], mhalf[:, 0:TILES], ALU.pow).then_inc(rstd2_s, 1)

            def low_w1(h):
                if h == 0:
                    pool.wait_ge(w1_hi_s, 1)
                ee = slice(h * HALF, (h + 1) * HALF)
                g.tensor_tensor(w1_lo[:, ee, :, :], w1[:, ee, :, :], w1_hi[:, ee, :, :].bitcast(fp32),
                                ALU.subtract).then_inc(w1_lo_s, 1)

            def set_w2():
                pool.wait_ge(w2_mean_s, 1)
                g.tensor_tensor(w2[:, :, :], w2[:, :, :], bc(w2_mean[:, :], 2, D), ALU.subtract).then_inc(w2_s, 1)

            def gated_ln(b):
                if b == 0:
                    pool.wait_ge(gates_s, 1)
                g.tensor_tensor(ln_gG[:, b, :, :], ln_g[:, :, :], bc(gates[:, b, 1, :], 1, EXPERTS), ALU.mult)
                g.tensor_tensor(ln_bG[:, b, :], ln_b[:, :], gates[0:EXPERTS, b, 1, :], ALU.mult).then_inc(lng_s, 1)

            def front(n):
                rstd_front(n)
                mask_q(n, 0)
                mask_q(n, 1)
                split_v(n, 0)
                split_v(n, 1)

            def body(i, att, ffn, nxt):
                n, f = i + 1, i - 1
                if nxt:
                    rstd_front(n)
                if att:
                    low_prob(i, 0)
                    low_prob(i, 1)
                if ffn:
                    coefficients(f, 0)
                if att:
                    low_prob(i, 2)
                if i == 0:
                    low_w1(0)
                if ffn:
                    coefficients(f, 1)
                if att:
                    low_prob(i, 3)
                if i == 0:
                    set_w2()
                    add_b_o(0)
                    low_w1(1)
                if nxt:
                    add_b_o(n)
                if ffn and att:
                    add_experts(f, 1)
                    add_experts(f, 0)
                if i == 1:
                    gated_ln(1)
                if att:
                    rstd_second(i)
                if nxt:
                    split_v(n, 0)
                if ffn:
                    coefficients(f, 2)
                if i == 0:
                    gated_ln(0)
                if nxt:
                    mask_q(n, 0)
                    mask_q(n, 1)
                if ffn:
                    coefficients(f, 3)
                if nxt:
                    split_v(n, 1)
                if ffn and att:
                    add_experts(f, 2)
                    add_experts(f, 3)
                if i == STEPS:
                    add_experts(f, 0)
                    add_experts(f, 2)

            steps(front, body)

        @block.scalar
        def _(act):
            a = nc.scalar
            act.wait_ge(loaded_mod, 16)
            act.wait_ge(set_pool, 1)
            a.activation(silu_den[:, :], cT[:, :], ACT.Exp, scale=-1.0).then_inc(set_act, 1)

            def hi_hT(n):
                act.wait_ge(xT_s, n + 1)
                if n > 0:
                    act.wait_ge(kq_proj, 6 * n)
                b = n // PER_BATCH
                a.activation(hT_hi[:, BLK:SPAN], U[0][:, 0:STEP], ACT.Identity, bias=modT[:, 0, b:b + 1],
                             scale=modT[:, 1, b:b + 1]).then_inc(hT_hi_s, 1)

            def double_hT(n):
                act.wait_ge(hT_s, n + 1)
                if n > 0:
                    act.wait_ge(v_proj, 2 * n)
                for part in range(2):
                    src = hT[:, part * BLK:part * BLK + STEP].rearrange("p (b k) -> p b k", k=BLK)
                    last = a.activation(hT2[:, :, :, part * BLK:(part + 1) * BLK], bc(src, 2, 2), ACT.Copy)
                last.then_inc(hT2_s, 1)

            def hi_k(n, g):
                act.wait_ge(kq_proj, 6 * n + g + 1)
                if g == 0:
                    if n > 0:
                        act.wait_ge(scored, 4 * n)
                a.activation(k_st[:, g, :], U[(g + 1) % 2][0:3 * GC, 0:SPAN], ACT.Identity,
                             bias=b_qk[:, 1, g:g + 1]).then_inc(kq_hi, 1)

            def hi_q(n, j):
                act.wait_ge(kq_proj, 6 * n + 5 + j)
                if j == 0:
                    if n > 0:
                        act.wait_ge(q_vec, 2 * n)
                    if n > 0:
                        act.wait_ge(q_pool, 2 * n)
                for g in (2 * j, 2 * j + 1):
                    last = a.activation(q_hl[:, g, :], U[0][0:3 * GC, (g % 2) * STEP:(g % 2 + 1) * STEP],
                                        ACT.Identity, bias=b_qk[:, 0, g:g + 1])
                last.then_inc(kq_hi, 1)

            def hi_v(n, j):
                act.wait_ge(v_proj, 2 * n + j + 1)
                if j == 0:
                    if n > 0:
                        act.wait_ge(pv_done, 4 * n)
                a.activation(v_parts[:, 4 * j:4 * j + 4, :, 0:DH].rearrange("p b h v -> p (b h) v"),
                             U[1][:, :].rearrange("p (n d) -> p n d", d=DH), ACT.Copy).then_inc(v_hi_s, 1)

            def exp(i, s):
                act.wait_ge(shifted, 4 * i + s + 1)
                if 4 * i + s - 3 > 0:
                    act.wait_ge(p_turned, 4 * i + s - 3)
                sd = sdif[:, s, :]
                a.activation(prob_hl[:, s, :, 0, :], by_key(sd), ACT.Exp, scale=float(DH) ** -0.5)
                if 4 * i + s - 3 > 0:
                    act.wait_ge(p_ready, 4 * i + s - 3)
                a.activation(prob[:, s, :], sd, ACT.Exp, scale=float(DH) ** -0.5).then_inc(exped, 1)

            def take_probT(i, s):
                act.wait_ge(p_turned, 4 * i + s + 1)
                if 4 * i + s - 1 > 0:
                    act.wait_ge(pv_done, 4 * i + s - 1)
                a.activation(probT[:, s % 2, :], probTB[:, :], ACT.Copy).then_inc(p_out, 1)

            def square(f, q):
                act.wait_ge(z_done, 4 * f + q + 1)
                if f > 0:
                    act.wait_ge(ss_s, 2 * f)
                a.activation(zsq[:, q % 2, :], z_bank(f, q)[:, :], ACT.Square).then_inc(sq_s, 1)

            def exp_weight(f):
                act.wait_ge(gdif_s, f + 1)
                a.activation(gexp[:, :], gdif[:, :], ACT.Exp).then_inc(gexp_s, 1)

            def square_sum(f, q):
                act.wait_ge(z_done, 4 * f + q + 1)
                if 4 * f + q - 1 > 0:
                    act.wait_ge(coef_s, 4 * f + q - 1)
                for e in range(HALF):
                    last = a.activation(zsq[:, q % 2, e * D:(e + 1) * D], z_bank(f, q)[:, e * D:(e + 1) * D], ACT.Square,
                                        accum_out=zss[:, q % 2, e:e + 1])
                last.then_inc(ss_act, 1)

            def gelu_table():
                a.activation(table[:, :], one[:, :], ACT.Gelu)

            def gelu(i, e):
                act.wait_ge(up_done, 8 * i + e + 1)
                if e == 0:
                    if i > 0:
                        act.wait_ge(z_done, 4 * i)
                for c in range(CH):
                    last = a.activation(hid[:, e, c, :], U[(e + 1) % 2][:, c * STEP:(c + 1) * STEP], ACT.Gelu,
                                        bias=b1[:, e, c:c + 1])
                last.then_inc(gelu_s, 1)

            def front(n):
                act.wait_ge(set_att, 1)
                hi_hT(n)
                hi_k(n, 0)
                hi_k(n, 1)
                double_hT(n)
                hi_k(n, 2)
                hi_k(n, 3)
                hi_v(n, 0)
                hi_q(n, 0)
                hi_v(n, 1)
                hi_q(n, 1)
                act.wait_ge(loaded_ffn, 16)
                a.activation(ones_r[:, :], ones[:, :], ACT.Copy)
                a.activation(center_r[:, :], center[:, :], ACT.Copy)
                act.wait_ge(loaded_f, ALL_F)
                a.activation(w1_hi[:, :, :, :], w1[:, :, :, :], ACT.Copy).then_inc(w1_hi_s, 1)

            def body(i, att, ffn, nxt):
                n, f = i + 1, i - 1
                if ffn:
                    exp_weight(f)
                if i == STEPS:
                    square_sum(f, 0)
                    square_sum(f, 1)
                    square_sum(f, 2)
                    square_sum(f, 3)
                if att:
                    exp(i, 0)
                    exp(i, 1)
                    exp(i, 2)
                if ffn and att:
                    square(f, 0)
                if att:
                    take_probT(i, 0)
                    exp(i, 3)
                if ffn and att:
                    square(f, 1)
                if nxt:
                    hi_hT(n)
                if att:
                    take_probT(i, 1)
                    take_probT(i, 2)
                if nxt:
                    double_hT(n)
                    hi_k(n, 0)
                    hi_k(n, 1)
                if att:
                    take_probT(i, 3)
                if nxt:
                    hi_k(n, 2)
                    hi_k(n, 3)
                    hi_v(n, 0)
                    hi_q(n, 0)
                if ffn and att:
                    square_sum(f, 2)
                if nxt:
                    hi_v(n, 1)
                    hi_q(n, 1)
                if att:
                    gelu_table()
                if ffn and att:
                    square_sum(f, 3)
                if att:
                    gelu(i, 0)
                    gelu(i, 1)
                    gelu(i, 2)
                    gelu(i, 3)
                    gelu(i, 4)
                    gelu(i, 5)
                    gelu(i, 6)
                    gelu(i, 7)

            steps(front, body)

        @block.vector
        def _(dve):
            v = nc.vector
            pre = Chain(dve, set_vec)
            cn, ca, cf = Chain(dve, v_front), Chain(dve, v_att), Chain(dve, v_ffn)

            def split(hi, lo, src):
                pre.link(v.tensor_copy(hi, src))
                return v.tensor_tensor(lo, src, hi.bitcast(fp32), ALU.subtract)

            def norm_stats(chain, at, mv):
                for tt in range(TILES):
                    last = v.bn_stats(stats[:, tt, :], X[:, at + tt, :])
                chain.link(last)
                for tt in range(TILES):
                    last = v.bn_aggr(mv[:, tt, :], stats[:, tt, :])
                return last

            def normed(dst, at, mv, rstd):
                for tt in range(TILES):
                    last = v.tensor_scalar(dst[:, tt, :], X[:, at + tt, :],
                                           mv[:, tt, 0:1], rstd[:, tt:tt + 1], ALU.subtract, ALU.mult)
                return last

            def stats_front(n):
                dve.wait_ge(loaded_x if n == 0 else loaded_rest, 16)
                norm_stats(cn, TILES * n, mv1).then_inc(stats1, 1)

            def normed_front(n):
                dve.wait_ge(rstd1_s, n + 1)
                if n > 0:
                    dve.wait_ge(xT_s, n)
                normed(xn1, TILES * n, mv1, rstd1).then_inc(xn1_s, 1)

            def take_hT(n):
                b = n // PER_BATCH
                if n > 0:
                    dve.wait_ge(hT2_s, n)
                if n == 0:
                    dve.wait_ge(set_pool, 1)
                cn.link(v.tensor_copy(hT[:, 0:BLK], hT[:, STEP:SPAN]))
                dve.wait_ge(hT_hi_s, n + 1)
                v.tensor_scalar(hT[:, BLK:SPAN], U[0][:, 0:STEP], modT[:, 1, b:b + 1],
                                modT[:, 0, b:b + 1], ALU.mult, ALU.add)
                cn.link(v.tensor_copy(hT_hi[:, 0:BLK], hT[:, 0:BLK]))
                v.tensor_tensor(hT_lo[:, :], hT[:, :], hT_hi[:, :].bitcast(fp32), ALU.subtract).then_inc(hT_s, 1)

            lk, lq = slice(2 * GC, 3 * GC), slice(GC, 2 * GC)

            def low_k(n, g):
                dve.wait_ge(kq_hi, 6 * n + g + 1)
                v.scalar_tensor_tensor(k_st[lk, g, :], U[(g + 1) % 2][lk, 0:SPAN], b_qk[lk, 1, g:g + 1],
                                       k_st[lk, g, :].bitcast(fp32), ALU.add, ALU.subtract).then_inc(k_ready, 1)

            def low_q(n, j):
                dve.wait_ge(kq_hi, 6 * n + 5 + j)
                for g in (2 * j, 2 * j + 1):
                    last = v.scalar_tensor_tensor(q_hl[lq, g, :], U[0][lq, (g % 2) * STEP:(g % 2 + 1) * STEP],
                                                  b_qk[lq, 0, g:g + 1], q_hl[lq, g, :].bitcast(fp32),
                                                  ALU.add, ALU.subtract)
                last.then_inc(q_lo_s, 1)

            def mask_q(n, j):
                dve.wait_ge(q_lo_s, 2 * n + j + 1)
                gg = slice(2 * j, 2 * j + 2)
                for h in range(HG - 1):
                    last = v.tensor_scalar(q_st[:, gg, :, h, :], blocks(q_hl[:, gg, :].bitcast(fp32)),
                                           headmask[:, h:h + 1], None, ALU.mult)
                last.then_inc(q_vec, 1)

            def rest_v(n, j):
                dve.wait_ge(v_hi_s, 2 * n + j + 1)
                if 2 * n + j - 1 > 0:
                    dve.wait_ge(v_ready, 2 * n + j - 1)
                v.tensor_tensor(v_rest[:, j, :].rearrange("p (n d) -> p n d", d=DH),
                                U[1][:, :].rearrange("p (n d) -> p n d", d=DH),
                                v_parts[:, 4 * j:4 * j + 4, :, 0:DH].rearrange("p b h v -> p (b h) v"),
                                ALU.subtract).then_inc(v_out, 1)

            def shift(i, s):
                dve.wait_ge(scored, 4 * i + s + 1)
                sc = by_key(scoreB[s % 2][:, :])
                ca.link(v.reduce_max(smax[:, s % 2, :], sc, axis=AX))
                if 4 * i + s - 3 > 0:
                    dve.wait_ge(exped, 4 * i + s - 3)
                v.tensor_tensor(by_key(sdif[:, s, :]), sc, bc(smax[:, s % 2, :], 2, KEYS),
                                ALU.subtract).then_inc(shifted, 1)

            def take_pv(i, s):
                dve.wait_ge(pv_done, 4 * i + s + 1)
                pv = M[:, 0:UNITS * VP].rearrange("p (u v) -> p u v", v=VP)
                v.reciprocal(rden[:, :], pv[:, :, VP - 1])
                v.tensor_reduce(num[:, :, :], pv[:, :, 0:VP - 1].rearrange("p u (a d) -> p u d a", a=3),
                                axis=AX, op=ALU.add).then_inc(pv_out, 1)
                dve.wait_ge(pv_out, 4 * i + s + 1)
                ca.link(v.tensor_tensor(attn[:, s * UNITS:(s + 1) * UNITS, :], num[:, :, :],
                                        bc(rden[:, :], 2, DH), ALU.mult))

            def weights(f):
                dve.wait_ge(gexp_s, f + 1)
                cf.link(v.tensor_scalar(gden[:, :], gexp[:, :], 1.0, None, ALU.add))
                cf.link(v.reciprocal(gw[:, :, 0], gden[:, :]))
                cf.link(v.tensor_tensor(gw[:, :, 1], gexp[:, :], gw[:, :, 0], ALU.mult))
                for tt in range(TILES):
                    for j in range(2):
                        last = v.tensor_scalar(wsel[:, tt, j, :], iota[:, :], gidf[:, tt, j:j + 1],
                                               gw[:, tt, j:j + 1], ALU.is_equal, ALU.mult)
                cf.link(last)
                if f > 0:
                    dve.wait_ge(coef_s, 4 * f)
                if f > 0:
                    dve.wait_ge(wT_done, f)
                v.tensor_tensor(wexp[:, :, :], wsel[:, :, 0, :], wsel[:, :, 1, :], ALU.add).then_inc(wexp_s, 1)

            def weights_T(f):
                dve.wait_ge(wT_done, f + 1)
                if f > 0:
                    dve.wait_ge(lnb_done, f)
                v.tensor_copy(wexpT[:, :], M[0:EXPERTS, 0:STEP]).then_inc(wT_out, 1)

            def add_ln_b(f):
                dve.wait_ge(lnb_done, f + 1)
                xs = X[:, TILES * f:TILES * (f + 1), :]
                v.tensor_tensor(xs, xs, M[:, 0:STEP].rearrange("p (a d) -> p a d", d=D), ALU.add).then_inc(lnb_out, 1)

            def zsum(f, q):
                dve.wait_ge(sq_s, 2 * f + q + 1)
                if 4 * f + q - 1 > 0:
                    dve.wait_ge(coef_s, 4 * f + q - 1)
                v.reduce_sum(zss[:, q % 2, :], zsq[:, q % 2, :].rearrange("p (e d) -> p e d", d=D),
                             axis=AX).then_inc(ss_s, 1)

            def scale(f, q):
                half, tt, b = q // 2, q % 2, f // PER_BATCH
                dve.wait_ge(coef_s, 4 * f + q + 1)
                if q == 0:
                    if f > 0:
                        dve.wait_ge(y_s, f)
                    if f == 0 or f == PER_BATCH:
                        dve.wait_ge(lng_s, b + 1)
                for e in range(HALF):
                    ee = half * HALF + e
                    last = v.scalar_tensor_tensor(ypart[:, tt, ee, :], z_bank(f, q)[:, e * D:(e + 1) * D],
                                                  zcoef[:, q % 2, e:e + 1], ln_gG[:, b, ee, :], ALU.mult, ALU.mult)
                last.then_inc(u_done, 1)

            def add_experts(f, q):
                half, tt = q // 2, q % 2
                at = half * HALF
                dve.wait_ge(u_done, 4 * f + q + 1)
                for n in (2, 1):
                    cf.link(v.tensor_tensor(ypart[:, tt, at:at + n, :], ypart[:, tt, at:at + n, :],
                                            ypart[:, tt, at + n:at + 2 * n, :], ALU.add))
                if half == 1:
                    cf.link(v.tensor_tensor(ypart[:, tt, 0, :], ypart[:, tt, 0, :], ypart[:, tt, at, :], ALU.add))
                    dve.wait_ge(stored, 16 * f)
                    v.tensor_tensor(yout[:, tt, :], ypart[:, tt, 0, :], X[:, TILES * f + tt, :],
                                    ALU.add).then_inc(y_s, 1)

            def top_two(i):
                dve.wait_ge(gate_done, i + 1)
                v.tensor_copy(gsc[:, :, :], M[:, 0:TILES * EXPERTS].rearrange("p (a e) -> p a e", e=EXPERTS)
                              ).then_inc(g_out, 1)
                dve.wait_ge(g_out, i + 1)
                for tt in range(TILES):
                    last = v.max(gtop[:, tt, :], gsc[:, tt, :])
                ca.link(last)
                for tt in range(TILES):
                    last = v.max_index(gidx[:, tt, :], gtop[:, tt, :], gsc[:, tt, :])
                ca.link(last)
                v.tensor_copy(gidf[:, :, :], gidx[:, :, 0:2])
                if i > 0:
                    dve.wait_ge(gexp_s, i)
                v.tensor_tensor(gdif[:, :], gtop[:, :, 1], gtop[:, :, 0], ALU.subtract).then_inc(gdif_s, 1)

            def turn_attn(i):
                ca.link(v.transpose(attnT[:, :], attn[:, :, :].rearrange("p n d -> p (n d)")))
                if i > 0:
                    dve.wait_ge(o_done, i)
                v.tensor_scalar(attnTb[:, :], attnT[:, :], b_v[:, :], None, ALU.add).then_inc(attn_ready, 1)

            def add_attn(i):
                dve.wait_ge(o_done, i + 1)
                dve.wait_ge(xb_s, i + 1)
                xs = X[:, TILES * i:TILES * (i + 1), :]
                v.tensor_tensor(xs, xs, M[:, 0:STEP].rearrange("p (a d) -> p a d", d=D), ALU.add).then_inc(x1_s, 1)
                dve.wait_ge(x1_s, i + 1)
                norm_stats(ca, TILES * i, mv2).then_inc(stats2, 1)

            def normed_second(i):
                dve.wait_ge(rstd2_s, i + 1)
                if i > 0:
                    dve.wait_ge(x2T_s, i)
                normed(xn2, TILES * i, mv2, rstd2).then_inc(xn2_s, 1)

            def take_h2T(i):
                b = i // PER_BATCH
                dve.wait_ge(x2T_s, i + 1)
                ca.link(v.tensor_scalar(h2T[:, :], M[:, 0:STEP], modT[:, 3, b:b + 1],
                                        modT[:, 2, b:b + 1], ALU.mult, ALU.add))
                ca.link(v.tensor_copy(h2_hi[:, i % 2, :], h2T[:, :]))
                v.tensor_tensor(h2_lo[:, i % 2, :], h2T[:, :], h2_hi[:, i % 2, :].bitcast(fp32),
                                ALU.subtract).then_inc(h2_s, 1)

            v.memset(idle[:, :], 0.0).then_inc(set_idle, 1)
            dve.wait_ge(loaded_mod, 16)
            dve.wait_ge(set_act, 1)
            pre.link(v.tensor_scalar(silu_den[:, :], silu_den[:, :], 1.0, None, ALU.add))
            pre.link(v.reciprocal(silu_den[:, :], silu_den[:, :]))
            v.tensor_tensor(silu[:, :], cT[:, :], silu_den[:, :], ALU.mult).then_inc(silu_s, 1)
            stats_front(0)
            dve.wait_ge(loaded_proj, 16)
            pre.link(split(w_qk_hi[:, :, :, :], w_qk_lo[:, :, :, :], w_qk[:, :, :, :]))
            normed_front(0)
            dve.wait_ge(set_pe, 2)
            mod_ps = M[:, 0:4 * BATCH].rearrange("p (j b) -> p j b", b=BATCH)
            v.tensor_scalar(modT[:, 0:4:2, :], mod_ps[:, 0:4:2, :], 0.0, None, ALU.add)
            v.tensor_scalar(modT[:, 1:4:2, :], mod_ps[:, 1:4:2, :], 1.0, None, ALU.add).then_inc(set_att, 1)
            dve.wait_ge(set_att, 1)

            def set_masks():
                dve.wait_ge(loaded_mask, 16)
                v.tensor_copy(ident16[:, :], ident[:, :])
                v.tensor_copy(rep16[:, :], rep[:, :])
                v.tensor_copy(mask16[:, :, :, :], maskf[:, :, :, :]).then_inc(mask_s, 1)

            gate_ps = zB[0][:, :].rearrange("p (b k d) -> p b k d", b=BATCH, k=2)
            flat = "p b k d -> p (b k d)"

            def set_gates_abs():
                v.tensor_scalar(gate_sign[:, :, :, :], gate_ps, 0.0, 2.0, ALU.is_ge, ALU.mult)
                pre.link(v.tensor_scalar(gates[:, :, :, :], gate_ps, -1.0, 0.25, ALU.mult, ALU.max))

            def set_gates():
                pre.link(v.tensor_tensor(gates[:, :, :, :], gate_ps, gates[:, :, :, :], ALU.max))
                v.scalar_tensor_tensor(gates[:, :, :, :].rearrange(flat), gate_sign[:, :, :, :].rearrange(flat),
                                       -1.0, gates[:, :, :, :].rearrange(flat), ALU.add, ALU.mult).then_inc(gates_s, 1)

            def gated_out():
                dve.wait_ge(gates_s, 1)
                dve.wait_ge(loaded_bo, 16)
                v.tensor_tensor(w_oG[:, :, :], bc(w_o[:, :], 1, BATCH), gates[:, :, 0, :], ALU.mult)
                v.tensor_tensor(b_oG[:, :, :], bc(b_o[:, :], 1, BATCH), gates[:, :, 0, :], ALU.mult).then_inc(b_o_s, 1)

            def set_ffn_bias():
                dve.wait_ge(loaded_f, ALL_F)
                pre.link(v.reduce_sum(b2_mean[:, :], b2[:, :], axis=AX))
                pre.link(v.tensor_scalar(b2_mean[:, :], b2_mean[:, :], 1.0 / D, None, ALU.mult))
                pre.link(v.tensor_scalar(b2[:, :], b2[:, :], b2_mean[:, :], None, ALU.subtract))
                split(b2_high[:, :], b2_low[:, :], b2[:, :]).then_inc(set_b2, 1)

            def set_w2_mean():
                pre.link(v.reduce_sum(w2_mean[:, :], w2[:, :, :], axis=AX))
                v.tensor_scalar(w2_mean[:, :], w2_mean[:, :], 1.0 / D, None, ALU.mult).then_inc(w2_mean_s, 1)

            def front(n):
                take_hT(n)
                set_masks()
                for g in range(GROUPS):
                    low_k(n, g)
                set_gates_abs()
                dve.wait_ge(loaded_att, 16)
                rest_v(n, 0)
                low_q(n, 0)
                mask_q(n, 0)
                rest_v(n, 1)
                low_q(n, 1)
                mask_q(n, 1)
                stats_front(n + 1)
                shift(n, 0)
                shift(n, 1)

            def body(i, att, ffn, nxt):
                n, f = i + 1, i - 1
                if att:
                    shift(i, 2)
                if ffn and att:
                    weights(f)
                if att:
                    shift(i, 3)
                if ffn and att:
                    zsum(f, 0)
                    weights_T(f)
                if nxt:
                    normed_front(n)
                if i == 0:
                    set_gates()
                if ffn and att:
                    add_ln_b(f)
                    scale(f, 0)
                    zsum(f, 1)
                if nxt:
                    take_hT(n)
                if att:
                    take_pv(i, 0)
                if i == 0:
                    set_w2_mean()
                if ffn and att:
                    scale(f, 1)
                if att:
                    take_pv(i, 1)
                if i == 0:
                    set_ffn_bias()
                if nxt:
                    low_k(n, 0)
                    low_k(n, 1)
                if i == 0:
                    gated_out()
                if att:
                    take_pv(i, 2)
                if nxt:
                    low_k(n, 2)
                    low_k(n, 3)
                if att:
                    take_pv(i, 3)
                    turn_attn(i)
                if nxt:
                    rest_v(n, 0)
                if att:
                    add_attn(i)
                if nxt:
                    low_q(n, 0)
                if att:
                    normed_second(i)
                if nxt:
                    rest_v(n, 1)
                if att:
                    take_h2T(i)
                if nxt:
                    low_q(n, 1)
                    mask_q(n, 0)
                    mask_q(n, 1)
                if ffn and att:
                    scale(f, 2)
                if att:
                    top_two(i)
                if ffn and att:
                    scale(f, 3)
                if i + 2 < STEPS:
                    stats_front(n + 1)
                if nxt:
                    shift(n, 0)
                    shift(n, 1)
                if i == STEPS:
                    weights(f)
                    weights_T(f)
                    scale(f, 0)
                    scale(f, 1)
                    add_ln_b(f)
                    scale(f, 2)
                    add_experts(f, 1)
                    scale(f, 3)
                    add_experts(f, 3)

            steps(front, body)

        @block.tensor
        def _(pe):
            mm, tr = nc.tensor.matmul, nc.tensor.transpose

            def three(outp, a_hi, a_lo, b_hi, b_lo):
                mm(outp, a_hi, b_hi, start=True, stop=False)
                mm(outp, a_hi, b_lo, start=False, stop=False)
                return mm(outp, a_lo, b_hi, start=False, stop=True)

            def keep_warm(count):
                for _ in range(count):
                    mm(zB[1][:, :], idle[:, 0:P], idle[:, :], start=True, stop=True)

            def keep_warm_last(count):
                pe.wait_ge(gelu_s, 8 * (STEPS - 1))
                for _ in range(count):
                    mm(U[1][:, :], idle[:, 0:P], idle[:, :], start=True, stop=True)

            pe.wait_ge(set_idle, 1)
            keep_warm(7)
            pe.wait_ge(loaded_mod, 16)
            pe.wait_ge(silu_s, 1)
            for n, j in enumerate((0, 1, 3, 4)):
                last = mm(M[:, n * BATCH:(n + 1) * BATCH], w_mod[:, j, :], silu[:, :], start=True, stop=True)
            last.then_inc(set_pe, 1)
            for b in range(BATCH):
                for n, j in enumerate((2, 5)):
                    at = (2 * b + n) * D
                    last = mm(zB[0][:, at:at + D], silu[:, b:b + 1].to_broadcast([P, P]), w_mod[:, j, :],
                              start=True, stop=True)
            last.then_inc(set_pe, 1)

            def turn_x(n):
                if n == 0:
                    pe.wait_ge(loaded_proj, 16)
                pe.wait_ge(xn1_s, n + 1)
                if 8 * n - 8 > 0:
                    pe.wait_ge(gelu_s, 8 * n - 8)
                for tt in range(TILES):
                    last = tr(U[0][:, tt * P:(tt + 1) * P], xn1[:, tt, :], ident[:, :])
                last.then_inc(xT_s, 1)

            def proj_k(n, g):
                if g == 0:
                    pe.wait_ge(hT_s, n + 1)
                if g > 1:
                    if 4 * n + g - 1 > 0:
                        pe.wait_ge(k_ready, 4 * n + g - 1)
                three(U[(g + 1) % 2][0:3 * GC, 0:SPAN], w_qk_hi[:, 1, g, :], w_qk_lo[:, 1, g, :], hT_hi[:, :],
                      hT_lo[:, :]).then_inc(kq_proj, 1)

            def proj_q(n, j):
                if j == 0:
                    pe.wait_ge(k_ready, 4 * n + 4)
                else:
                    pe.wait_ge(q_lo_s, 2 * n + 1)
                for g in (2 * j, 2 * j + 1):
                    last = three(U[0][0:3 * GC, (g % 2) * STEP:(g % 2 + 1) * STEP], w_qk_hi[:, 0, g, :],
                                 w_qk_lo[:, 0, g, :], hT_hi[:, BLK:SPAN], hT_lo[:, BLK:SPAN])
                last.then_inc(kq_proj, 1)

            def proj_v(n, j):
                if j == 0:
                    pe.wait_ge(hT2_s, n + 1)
                    pe.wait_ge(k_ready, 4 * n + 3)
                else:
                    pe.wait_ge(v_out, 2 * n + 1)
                for m in range(4):
                    last = mm(U[1][:, m * D:(m + 1) * D], hT2[:, 4 * j + m, :, :].rearrange("p r k -> p (r k)"),
                              w_v[:, :], start=True, stop=True)
                last.then_inc(v_proj, 1)

            def up(i, e, nxt):
                if e == 0:
                    if i == 0:
                        pe.wait_ge(w1_lo_s, 2)
                    pe.wait_ge(h2_s, i + 1)
                if e < 2 and nxt:
                    if e == 0:
                        pe.wait_ge(v_out, 2 * i + 4)
                    else:
                        pe.wait_ge(q_lo_s, 2 * i + 4)
                elif e < 2:
                    if i > 0:
                        pe.wait_ge(gelu_s, 8 * i)
                else:
                    if 8 * i + e - 1 > 0:
                        pe.wait_ge(gelu_s, 8 * i + e - 1)
                for c in range(CH):
                    last = three(U[(e + 1) % 2][:, c * STEP:(c + 1) * STEP], w1_hi[:, e, c, :], w1_lo[:, e, c, :],
                                 h2_hi[:, i % 2, :], h2_lo[:, i % 2, :])
                last.then_inc(up_done, 1)

            def scores(i, s):
                if s == 0:
                    pe.wait_ge(k_ready, 4 * i + 4)
                    pe.wait_ge(q_vec, 2 * i + 2)
                    pe.wait_ge(q_pool, 2 * i + 2)
                if 4 * i + s - 1 > 0:
                    pe.wait_ge(shifted, 4 * i + s - 1)
                which = mask16[:, i if s == 0 else STEPS, :, :]
                bank = scoreB[s % 2]
                mm(bank[:, :].rearrange("p (b g k) -> p b g k", b=2, g=GROUPS), rep16[:, :],
                   bc(which, 2, GROUPS), start=True, stop=False, skip_group_check=True)
                for u in range(UNITS):
                    blk, g = 2 * s + u // GROUPS, u % GROUPS
                    last = mm(bank[:, u * KEYS:(u + 1) * KEYS], q_st[:, g, blk, :, :].rearrange("p h q -> p (h q)"),
                              k_st[:, g, blk * BLK:blk * BLK + KEYS], start=False, stop=u == UNITS - 1,
                              skip_group_check=True)
                last.then_inc(scored, 1)

            def turn(i, s):
                pe.wait_ge(p_ready, 4 * i + s + 1)
                if 4 * i + s > 0:
                    pe.wait_ge(p_out, 4 * i + s)
                for u in range(UNITS):
                    last = tr(probTB[:, u * P:(u + 1) * P],
                              prob_hl[:, s, u, :, :].rearrange("p a k -> p (a k)"), ident16[:, :])
                last.then_inc(p_turned, 1)

            def values(i, s):
                pe.wait_ge(p_out, 4 * i + s + 1)
                pe.wait_ge(v_ready, 2 * i + 1 + s // 2)
                if s > 0:
                    if 4 * i + s > 0:
                        pe.wait_ge(pv_out, 4 * i + s)
                elif i > 0:
                    if i > 0:
                        pe.wait_ge(lnb_out, i)
                for u in range(UNITS):
                    blk, g = 2 * s + u // GROUPS, u % GROUPS
                    for h in range(HG):
                        last = mm(M[h * BLK:(h + 1) * BLK, u * VP:(u + 1) * VP],
                                  probT[:, s % 2, u * P + h * BLK:u * P + (h + 1) * BLK],
                                  v_parts[:, blk, HG * g + h, :], start=True, stop=True)
                last.then_inc(pv_done, 1)

            def down(f, q, part):
                half, tt = q // 2, q % 2
                if part == 0:
                    down_start(f, q)
                for e in range(part * HALF // 2, (part + 1) * HALF // 2):
                    ee = half * HALF + e
                    for c in range(CH):
                        last = mm(z_bank(f, q)[:, e * D:(e + 1) * D], hid[:, ee, c, tt * P:(tt + 1) * P],
                                  w2[:, ee * CH + c, :], start=False, stop=e == HALF - 1 and c == CH - 1,
                                  skip_group_check=True)
                if part == 1:
                    last.then_inc(z_done, 1)

            def down_start(f, q):
                if f == 0 and q == 0:
                    pe.wait_ge(w2_s, 1)
                    pe.wait_ge(b2_moved, 32)
                half, tt = q // 2, q % 2
                pe.wait_ge(gelu_s, 8 * f + HALF * (half + 1))
                if f == STEPS - 1 and q > 1:
                    pe.wait_ge(shifted, 4 * STEPS)
                else:
                    if 4 * f + q - 1 > 0:
                        pe.wait_ge(u_done, 4 * f + q - 1)
                bank, tok = z_bank(f, q), slice(tt * P, (tt + 1) * P)
                by_e = bank[:, :].rearrange("p (e d) -> p e d", d=D)
                mm(by_e, h2_hi[:, f % 2, tok], bc(center_r[:, :], 1, HALF), start=True, stop=False, skip_group_check=True)
                mm(by_e, h2_lo[:, f % 2, tok], bc(center_r[:, :], 1, HALF), start=False, stop=False, skip_group_check=True)
                mm(by_e, ones_r[:, :], b2_rows[:, half * HALF:(half + 1) * HALF, :], start=False, stop=False,
                   skip_group_check=True)

            def turn_weights(f):
                pe.wait_ge(wexp_s, f + 1)
                for tt in range(TILES):
                    last = tr(M[0:EXPERTS, tt * P:(tt + 1) * P], wexp[:, tt, :], ident[:, :])
                last.then_inc(wT_done, 1)

            def ln_b_sum(f):
                if f == 0 or f == PER_BATCH:
                    pe.wait_ge(lng_s, f // PER_BATCH + 1)
                pe.wait_ge(wT_out, f + 1)
                for tt in range(TILES):
                    last = mm(M[:, tt * D:(tt + 1) * D], wexpT[:, tt * P:(tt + 1) * P], ln_bG[:, f // PER_BATCH, :],
                              start=True, stop=True)
                last.then_inc(lnb_done, 1)

            def out_proj(i):
                pe.wait_ge(attn_ready, i + 1)
                for tt in range(TILES):
                    last = mm(M[:, tt * D:(tt + 1) * D], attnTb[:, tt * P:(tt + 1) * P], w_oG[:, i // PER_BATCH, :],
                              start=True, stop=True)
                last.then_inc(o_done, 1)

            def turn_x2(i):
                pe.wait_ge(xn2_s, i + 1)
                for tt in range(TILES):
                    last = tr(M[:, tt * P:(tt + 1) * P], xn2[:, tt, :], ident[:, :])
                last.then_inc(x2T_s, 1)

            def gate(i):
                pe.wait_ge(h2_s, i + 1)
                for tt in range(TILES):
                    last = mm(M[:, tt * EXPERTS:(tt + 1) * EXPERTS], h2T[:, tt * P:(tt + 1) * P], w_gate[:, :],
                              start=True, stop=True)
                last.then_inc(gate_done, 1)

            def front(n):
                turn_x(n)
                keep_warm(8)
                proj_k(n, 0)
                proj_k(n, 1)
                keep_warm(2)
                proj_k(n, 2)
                proj_k(n, 3)
                pe.wait_ge(loaded_att, 16)
                keep_warm(3)
                proj_v(n, 0)
                proj_q(n, 0)
                proj_v(n, 1)
                proj_q(n, 1)
                keep_warm(12)
                pe.wait_ge(mask_s, 1)
                scores(n, 0)
                scores(n, 1)

            def body(i, att, ffn, nxt):
                n, f = i + 1, i - 1
                if i == 0:
                    keep_warm(2)
                if att:
                    scores(i, 2)
                if ffn and att:
                    down(f, 0, 0)
                    down(f, 0, 1)
                if i == 0:
                    keep_warm(2)
                if att:
                    scores(i, 3)
                if i == 0:
                    keep_warm(5)
                if att:
                    turn(i, 0)
                if ffn:
                    turn_weights(f)
                if i == STEPS:
                    down(f, 3, 0)
                    down(f, 3, 1)
                if ffn and att:
                    down(f, 1, 0)
                    down(f, 1, 1)
                if ffn:
                    ln_b_sum(f)
                if i == 0:
                    keep_warm(3)
                    keep_warm(3)
                if nxt:
                    turn_x(n)
                if i == 0:
                    keep_warm(2)
                if att:
                    turn(i, 1)
                    values(i, 0)
                if i == STEPS - 1:
                    keep_warm_last(2)
                if att:
                    turn(i, 2)
                if ffn and att:
                    down(f, 2, 0)
                if att:
                    values(i, 1)
                if i == STEPS - 1:
                    keep_warm_last(2)
                if i == 0:
                    keep_warm(3)
                if nxt:
                    proj_k(n, 0)
                    proj_k(n, 1)
                if att:
                    turn(i, 3)
                    values(i, 2)
                if i == STEPS - 1:
                    keep_warm_last(3)
                if nxt:
                    proj_k(n, 2)
                    proj_k(n, 3)
                if att:
                    values(i, 3)
                if ffn and att:
                    down(f, 2, 1)
                if nxt:
                    proj_v(n, 0)
                    proj_q(n, 0)
                if i == STEPS - 1:
                    keep_warm_last(5)
                if att:
                    out_proj(i)
                if ffn and att:
                    down(f, 3, 0)
                if nxt:
                    proj_v(n, 1)
                    proj_q(n, 1)
                if i == STEPS - 1:
                    keep_warm_last(4)
                if att:
                    turn_x2(i)
                if ffn and att:
                    down(f, 3, 1)
                if i == 0:
                    keep_warm(1)
                if att:
                    up(i, 0, nxt)
                    up(i, 1, nxt)
                    gate(i)
                    up(i, 2, nxt)
                    up(i, 3, nxt)
                    up(i, 4, nxt)
                if nxt:
                    scores(n, 0)
                if att:
                    up(i, 5, nxt)
                if i == STEPS - 1:
                    down(i, 0, 0)
                if att:
                    up(i, 6, nxt)
                if i == STEPS - 1:
                    down(i, 0, 1)
                if nxt:
                    scores(n, 1)
                if att:
                    up(i, 7, nxt)
                if i == STEPS - 1:
                    down(i, 1, 0)
                    down(i, 1, 1)
                    down(i, 2, 0)
                    down(i, 2, 1)

            steps(front, body)


def kernel(**inputs):
    import concourse.bacc as bacc
    from concourse.bass_utils import run_bass_kernel_spmd

    def a(name):
        return np.asarray(inputs["L0_" + name])

    def by_group(w):
        w = w.reshape(w.shape[0], GROUPS, 1, GC)
        return np.broadcast_to(w, (w.shape[0], GROUPS, 3, GC)).reshape(w.shape[0], GROUPS, 3 * GC)

    order = np.arange(D).reshape(GROUPS, HG, DH).transpose(1, 0, 2).reshape(D)
    w_qk = np.stack([by_group(a("attn_q_w").T), by_group(a("attn_k_w").T)], 1)
    b_qk = np.stack([by_group(a("attn_q_b")[None]), by_group(a("attn_k_b")[None])], 1)[0].transpose(2, 0, 1)
    j, k = np.arange(BLK)[:, None], np.arange(KEYS)[None, :]
    inner = np.where((k > j) & (k <= j + BLK), 0.0, -1e30)
    first = np.where((k > j) & (k <= j + BLK) & (k >= BLK), 0.0, -1e30)
    masks = np.stack([np.stack([first if s % PER_BATCH == 0 and s < STEPS else inner, inner], 1)
                      for s in range(STEPS + 1)], 1)
    f4 = np.float32
    arrays = {
        "x": a("attn_x"), "w_qk": w_qk, "b_qk": b_qk, "w_v": a("attn_v_w").T,
        "b_v": a("attn_v_b")[order][:, None], "w_o": a("attn_o_w").T[order], "b_o": a("attn_o_b"),
        "w_mod": a("wmod").reshape(D, 6, D), "cT": a("c").T,
        "ident": np.eye(P, dtype=f4), "rep": np.tile(np.eye(BLK, dtype=f4), (1, HG)), "masks": masks.astype(f4),
        "headmask": (np.arange(3 * GC)[:, None] % GC // DH == np.arange(HG)[None, :]).astype(f4),
        "iota": np.broadcast_to(np.arange(EXPERTS, dtype=f4), (P, EXPERTS)),
        "center": (np.eye(D) - 1.0 / D).astype(f4),
        "w_gate": a("ffn_gate_w"), "w1": a("ffn_w1").reshape(EXPERTS, D, CH, P).transpose(1, 0, 2, 3),
        "b1": a("ffn_b1").reshape(EXPERTS, CH, P).transpose(2, 0, 1),
        "w2": a("ffn_w2").reshape(EXPERTS * CH, P, D).transpose(1, 0, 2), "b2": a("ffn_b2"),
        "ln_g": a("ffn_ln_g"), "ln_b": a("ffn_ln_b"),
    }

    def pack(rows, *names):
        cols = [arrays.pop(name) for name in names]
        return np.concatenate([np.concatenate([c.reshape(c.shape[0], -1), np.zeros((rows - c.shape[0], c[0].size), f4)])
                               for c in cols], 1)

    arrays.update(
        pack_mod=pack(P, "cT", "w_mod"), pack_proj=pack(P, "ident", "b_qk", "w_qk"),
        pack_att=pack(P, "w_v", "headmask", "b_v", "w_o"), pack_mask=pack(BLK, "rep", "masks"),
        pack_ffn=pack(P, "center", "iota", "w_gate", "b1"))
    arrays = {name: np.ascontiguousarray(x) for name, x in arrays.items()}
    nc = bacc.Bacc("TRN2", target_bir_lowering=False, num_devices=1)
    dram = {name: nc.dram_tensor(f"in_{name}", x.shape, mybir.dt.from_np(x.dtype), kind="ExternalInput").ap()
            for name, x in arrays.items()}
    out = nc.dram_tensor("out_x", (BATCH, SEQ, D), mybir.dt.float32, kind="ExternalOutput").ap()
    build(nc, dram, out)
    r = run_bass_kernel_spmd(nc, [{f"in_{name}": x for name, x in arrays.items()}], core_ids=[0])
    return r.results[0]["out_x"]
```
